# Optimizing a Trainium2 kernel written in Bass

```python
import numpy as np
import jax
import jax.numpy as jnp

def _softmax(x, axis=-1):
    return jax.nn.softmax(x, axis=axis)

def _gelu(x):
    return jax.nn.gelu(x, approximate=True)

def _silu(x):
    return jax.nn.silu(x)

def _sigmoid(x):
    return jax.nn.sigmoid(x)

def _layernorm(x, axis=-1, eps=1e-05):
    m = jnp.mean(x, axis=axis, keepdims=True)
    v = jnp.var(x, axis=axis, keepdims=True)
    return (x - m) / jnp.sqrt(v + eps)

def _scatter_add(tgt, idx, src, axis=0):
    return tgt.at[idx].add(src)

def _segment_sum(src, seg, n):
    return jax.ops.segment_sum(src, seg, n)
kernel_name = 'mk_gnn_resnorm_d4_gnn_r32_91e878'

def setup_inputs(seed: int=0):
    np.random.seed(seed)
    _w = jnp.asarray

    def _rec_inputs():
        import jax
        import jax.numpy as jnp
        _gk = jax.random.key(seed)
        x = -0.0003713 + 1 * jax.random.normal(jax.random.fold_in(_gk, 1), (3125, 128), jnp.float32)
        _s = jax.random.randint(jax.random.fold_in(_gk, 2), (25000,), 0, 3125, jnp.int32)
        _d = jax.random.randint(jax.random.fold_in(_gk, 3), (25000,), 0, 3125, jnp.int32)
        _loop = jnp.arange(3125, dtype=jnp.int32)
        src = jnp.concatenate([_s, _d, _loop])
        dst = jnp.concatenate([_d, _s, _loop])
        _o = jnp.argsort(dst, stable=True)
        src = src[_o]
        dst = dst[_o]
        edge_attr_16 = 0.000189758 + 1.00013 * jax.random.normal(jax.random.fold_in(_gk, 11), (53125, 16), jnp.float32)
        edge_type_8 = jax.random.randint(jax.random.fold_in(_gk, 13), (53125,), 0, 8, jnp.int32)
        return (x, src, dst, edge_attr_16, edge_type_8)
    x, src, dst, edge_attr_16, edge_type_8 = _rec_inputs()

    def _L0_gnn_setup():
        import jax, jax.numpy as jnp
        import numpy as np
        N_NODES = 3125
        N_EDGES = 18750
        H = 128
        T = 8
        L = 2

        def _gru_cell(x, h, wih, whh, bih, bhh):
            gi = x @ wih.T + bih
            gh = h @ whh.T + bhh
            i_r, i_z, i_n = jnp.split(gi, 3, axis=-1)
            h_r, h_z, h_n = jnp.split(gh, 3, axis=-1)
            r = jax.nn.sigmoid(i_r + h_r)
            z = jax.nn.sigmoid(i_z + h_z)
            n = jnp.tanh(i_n + r * h_n)
            return (1.0 - z) * n + z * h
        key = jax.random.key(seed)
        ks = jax.random.split(key, 12)
        s = 1.0 / np.sqrt(H)
        inp = {'node_features': jax.random.normal(ks[0], (N_NODES, H), dtype=jnp.float32), 'edge_index': jax.random.randint(ks[1], (2, N_EDGES), 0, N_NODES, dtype=jnp.int64), 'edge_type': jax.random.randint(ks[2], (N_EDGES,), 0, T, dtype=jnp.int64), 'node_proj_w': jax.random.uniform(ks[3], (H, H), jnp.float32, -s, s), 'node_proj_b': jax.random.uniform(ks[4], (H,), jnp.float32, -s, s), 'edge_W': jax.random.uniform(ks[5], (L, T, H, H), jnp.float32, -s, s), 'edge_b': jax.random.uniform(ks[6], (L, T, H), jnp.float32, -s, s), 'gru_wih': jax.random.uniform(ks[7], (L, 3 * H, H), jnp.float32, -s, s), 'gru_whh': jax.random.uniform(ks[8], (L, 3 * H, H), jnp.float32, -s, s), 'gru_bih': jax.random.uniform(ks[9], (L, 3 * H), jnp.float32, -s, s), 'gru_bhh': jax.random.uniform(ks[10], (L, 3 * H), jnp.float32, -s, s), 'out_w': jax.random.uniform(ks[11], (H, H), jnp.float32, -s, s), 'out_b': jnp.zeros((H,), jnp.float32)}
        return inp
    _L0_gnn_all = _L0_gnn_setup()
    _L0_gnn_in = {k: v for k, v in _L0_gnn_all.items() if k in ('node_proj_w', 'node_proj_b', 'edge_W', 'edge_b', 'gru_wih', 'gru_whh', 'gru_bih', 'gru_bhh', 'out_w', 'out_b')}
    del _L0_gnn_all

    def _L1_gnn_setup():
        import jax, jax.numpy as jnp
        import numpy as np
        N, E, D, R = (50000, 18750, 128, 8)

        def rgcn_conv(x, src, dst, etype, W, root, bias):
            n = x.shape[0]
            r = W.shape[0]
            xw = jnp.einsum('nd,rdo->rno', x, W)
            seg = etype * n + dst
            counts = jax.ops.segment_sum(jnp.ones(src.shape, dtype=x.dtype), seg, num_segments=r * n)
            norm = 1.0 / jnp.maximum(counts[seg], 1.0)
            msg = xw[etype, src] * norm[:, None]
            agg = jax.ops.segment_sum(msg, dst, num_segments=n)
            return agg + x @ root + bias
        key = jax.random.key(seed)
        ks = jax.random.split(key, 16)
        s = 1.0 / np.sqrt(D)
        inp = {'x': jax.random.normal(ks[0], (N, D), dtype=jnp.float32), 'edge_index': jax.random.randint(ks[1], (2, E), 0, N, dtype=jnp.int32), 'edge_type': jax.random.randint(ks[2], (E,), 0, R, dtype=jnp.int32), 'W1': jax.random.normal(ks[3], (R, D, D), dtype=jnp.float32) * s, 'root1': jax.random.normal(ks[4], (D, D), dtype=jnp.float32) * s, 'b1': jnp.zeros((D,), dtype=jnp.float32), 'W2': jax.random.normal(ks[5], (R, D, D), dtype=jnp.float32) * s, 'root2': jax.random.normal(ks[6], (D, D), dtype=jnp.float32) * s, 'b2': jnp.zeros((D,), dtype=jnp.float32), 'W3': jax.random.normal(ks[7], (R, D, D), dtype=jnp.float32) * s, 'root3': jax.random.normal(ks[8], (D, D), dtype=jnp.float32) * s, 'b3': jnp.zeros((D,), dtype=jnp.float32), 'res_w': jax.random.normal(ks[9], (D, D), dtype=jnp.float32) * s, 'res_b': jnp.zeros((D,), dtype=jnp.float32)}
        return inp
    _L1_gnn_all = _L1_gnn_setup()
    _L1_gnn_in = {k: v for k, v in _L1_gnn_all.items() if k in ('W1', 'root1', 'b1', 'W2', 'root2', 'b2', 'W3', 'root3', 'b3', 'res_w', 'res_b')}
    del _L1_gnn_all

    def _L2_gnn_setup():
        import jax, jax.numpy as jnp
        import numpy as np
        N_NODES = 50000
        N_EDGES = 18750
        IN_CH = 128
        OUT_CH = 128
        key = jax.random.key(seed)
        k1, k2, k3, k4 = jax.random.split(key, 4)
        x = jax.random.normal(k1, (N_NODES, IN_CH), dtype=jnp.float32)
        edge_index = jax.random.randint(k2, (2, N_EDGES), 0, N_NODES, dtype=jnp.int64)
        W = jax.random.normal(k3, (OUT_CH, IN_CH), dtype=jnp.float32) * (1.0 / np.sqrt(IN_CH))
        b = jax.random.normal(k4, (OUT_CH,), dtype=jnp.float32) * 0.01
        return {'x': x, 'edge_index': edge_index, 'W': W, 'b': b}
    _L2_gnn_all = _L2_gnn_setup()
    _L2_gnn_in = {k: v for k, v in _L2_gnn_all.items() if k in ('W', 'b')}
    del _L2_gnn_all

    def _L3_gnn_setup():
        import jax, jax.numpy as jnp
        import numpy as np
        NEG_SLOPE = 0.01

        def _scatter_mean(vals, idx, num_segments):
            s = jax.ops.segment_sum(vals, idx, num_segments=num_segments)
            cnt = jax.ops.segment_sum(jnp.ones((vals.shape[0],), vals.dtype), idx, num_segments=num_segments)
            return s / jnp.maximum(cnt, 1.0)[:, None]
        key = jax.random.key(seed)
        ks = jax.random.split(key, 8)
        N, E = (3125, 100000)
        node_emb, edge_emb = (128, 16)
        d_in = node_emb + 2 * edge_emb
        x = jax.random.normal(ks[0], (N, node_emb), dtype=jnp.float32)
        edge_index = jax.random.randint(ks[1], (2, E), 0, N, dtype=jnp.int32)
        edge_attr = jax.random.normal(ks[2], (E, edge_emb), dtype=jnp.float32)
        W1 = jax.random.normal(ks[3], (d_in, node_emb), dtype=jnp.float32) * (1.0 / np.sqrt(d_in))
        b1 = jax.random.normal(ks[4], (node_emb,), dtype=jnp.float32) * 0.01
        W2 = jax.random.normal(ks[5], (node_emb, node_emb), dtype=jnp.float32) * (1.0 / np.sqrt(node_emb))
        b2 = jax.random.normal(ks[6], (node_emb,), dtype=jnp.float32) * 0.01
        return {'x': x, 'edge_index': edge_index, 'edge_attr': edge_attr, 'W1': W1, 'b1': b1, 'W2': W2, 'b2': b2}
    _L3_gnn_all = _L3_gnn_setup()
    _L3_gnn_in = {k: v for k, v in _L3_gnn_all.items() if k in ('W1', 'b1', 'W2', 'b2')}
    del _L3_gnn_all
    return {'x': x, 'src': src, 'dst': dst, 'edge_attr_16': edge_attr_16, 'edge_type_8': edge_type_8, 'L0_gnn_node_proj_w': _L0_gnn_in['node_proj_w'], 'L0_gnn_node_proj_b': _L0_gnn_in['node_proj_b'], 'L0_gnn_edge_W': _L0_gnn_in['edge_W'], 'L0_gnn_edge_b': _L0_gnn_in['edge_b'], 'L0_gnn_gru_wih': _L0_gnn_in['gru_wih'], 'L0_gnn_gru_whh': _L0_gnn_in['gru_whh'], 'L0_gnn_gru_bih': _L0_gnn_in['gru_bih'], 'L0_gnn_gru_bhh': _L0_gnn_in['gru_bhh'], 'L0_gnn_out_w': _L0_gnn_in['out_w'], 'L0_gnn_out_b': _L0_gnn_in['out_b'], 'L1_gnn_W1': _L1_gnn_in['W1'], 'L1_gnn_root1': _L1_gnn_in['root1'], 'L1_gnn_b1': _L1_gnn_in['b1'], 'L1_gnn_W2': _L1_gnn_in['W2'], 'L1_gnn_root2': _L1_gnn_in['root2'], 'L1_gnn_b2': _L1_gnn_in['b2'], 'L1_gnn_W3': _L1_gnn_in['W3'], 'L1_gnn_root3': _L1_gnn_in['root3'], 'L1_gnn_b3': _L1_gnn_in['b3'], 'L1_gnn_res_w': _L1_gnn_in['res_w'], 'L1_gnn_res_b': _L1_gnn_in['res_b'], 'L2_gnn_W': _L2_gnn_in['W'], 'L2_gnn_b': _L2_gnn_in['b'], 'L3_gnn_W1': _L3_gnn_in['W1'], 'L3_gnn_b1': _L3_gnn_in['b1'], 'L3_gnn_W2': _L3_gnn_in['W2'], 'L3_gnn_b2': _L3_gnn_in['b2']}

def reference(x, src, dst, edge_attr_16, edge_type_8, L0_gnn_node_proj_w, L0_gnn_node_proj_b, L0_gnn_edge_W, L0_gnn_edge_b, L0_gnn_gru_wih, L0_gnn_gru_whh, L0_gnn_gru_bih, L0_gnn_gru_bhh, L0_gnn_out_w, L0_gnn_out_b, L1_gnn_W1, L1_gnn_root1, L1_gnn_b1, L1_gnn_W2, L1_gnn_root2, L1_gnn_b2, L1_gnn_W3, L1_gnn_root3, L1_gnn_b3, L1_gnn_res_w, L1_gnn_res_b, L2_gnn_W, L2_gnn_b, L3_gnn_W1, L3_gnn_b1, L3_gnn_W2, L3_gnn_b2):
    import jax
    import jax.numpy as jnp

    def _L0_gnn_ref(node_features, edge_index, edge_type, node_proj_w, node_proj_b, edge_W, edge_b, gru_wih, gru_whh, gru_bih, gru_bhh, out_w, out_b):
        import jax, jax.numpy as jnp
        import numpy as np
        N_NODES = 3125
        N_EDGES = 18750
        H = 128
        T = 8
        L = 2

        def _gru_cell(x, h, wih, whh, bih, bhh):
            gi = x @ wih.T + bih
            gh = h @ whh.T + bhh
            i_r, i_z, i_n = jnp.split(gi, 3, axis=-1)
            h_r, h_z, h_n = jnp.split(gh, 3, axis=-1)
            r = jax.nn.sigmoid(i_r + h_r)
            z = jax.nn.sigmoid(i_z + h_z)
            n = jnp.tanh(i_n + r * h_n)
            return (1.0 - z) * n + z * h
        num_nodes = node_features.shape[0]
        src, dst = (edge_index[0], edge_index[1])
        h = jax.nn.relu(node_features @ node_proj_w.T + node_proj_b)
        for l in range(L):
            trans = jnp.einsum('nh,tdh->tnd', h, edge_W[l])
            msgs = trans[edge_type, src]
            agg = jax.ops.segment_sum(msgs, dst, num_segments=num_nodes)
            h = _gru_cell(agg, h, gru_wih[l], gru_whh[l], gru_bih[l], gru_bhh[l])
            h = jax.nn.relu(h)
        return h @ out_w.T + out_b

    def _L1_gnn_ref(x, edge_index, edge_type, W1, root1, b1, W2, root2, b2, W3, root3, b3, res_w, res_b):
        import jax, jax.numpy as jnp
        import numpy as np
        N, E, D, R = (50000, 18750, 128, 8)

        def rgcn_conv(x, src, dst, etype, W, root, bias):
            n = x.shape[0]
            r = W.shape[0]
            xw = jnp.einsum('nd,rdo->rno', x, W)
            seg = etype * n + dst
            counts = jax.ops.segment_sum(jnp.ones(src.shape, dtype=x.dtype), seg, num_segments=r * n)
            norm = 1.0 / jnp.maximum(counts[seg], 1.0)
            msg = xw[etype, src] * norm[:, None]
            agg = jax.ops.segment_sum(msg, dst, num_segments=n)
            return agg + x @ root + bias
        src, dst = (edge_index[0], edge_index[1])
        res = x @ res_w + res_b
        h = jax.nn.relu(rgcn_conv(x, src, dst, edge_type, W1, root1, b1))
        h = res + jax.nn.relu(h)
        h = jax.nn.relu(rgcn_conv(h, src, dst, edge_type, W2, root2, b2))
        h = res + jax.nn.relu(h)
        h = jax.nn.relu(rgcn_conv(h, src, dst, edge_type, W3, root3, b3))
        h = res + jax.nn.relu(h)
        return h

    def _L2_gnn_ref(x, edge_index, W, b):
        import jax, jax.numpy as jnp
        import numpy as np
        N_NODES = 50000
        N_EDGES = 18750
        IN_CH = 128
        OUT_CH = 128
        row, col = (edge_index[0], edge_index[1])
        n = x.shape[0]
        deg = jax.ops.segment_sum(jnp.ones_like(row, dtype=x.dtype), row, num_segments=n)
        deg_inv_sqrt = jnp.where(deg > 0, jax.lax.rsqrt(jnp.where(deg > 0, deg, 1.0)), 0.0)
        norm = deg_inv_sqrt[row] * deg_inv_sqrt[col]
        msgs = norm[:, None] * x[col]
        agg = jax.ops.segment_sum(msgs, row, num_segments=n)
        return agg @ W.T + b

    def _L3_gnn_ref(x, edge_index, edge_attr, W1, b1, W2, b2):
        import jax, jax.numpy as jnp
        import numpy as np
        NEG_SLOPE = 0.01

        def _scatter_mean(vals, idx, num_segments):
            s = jax.ops.segment_sum(vals, idx, num_segments=num_segments)
            cnt = jax.ops.segment_sum(jnp.ones((vals.shape[0],), vals.dtype), idx, num_segments=num_segments)
            return s / jnp.maximum(cnt, 1.0)[:, None]
        N = x.shape[0]
        row, col = (edge_index[0], edge_index[1])
        rec_attr = _scatter_mean(edge_attr, row, N)
        sent_attr = _scatter_mean(edge_attr, col, N)
        out = jnp.concatenate([x, rec_attr, sent_attr], axis=1)
        h = out @ W1 + b1
        h = jnp.where(h >= 0, h, NEG_SLOPE * h)
        return h @ W2 + b2
    edge_index = jnp.stack([src, dst])
    x = _layernorm(x + _L0_gnn_ref(x, edge_index, edge_type_8, L0_gnn_node_proj_w, L0_gnn_node_proj_b, L0_gnn_edge_W, L0_gnn_edge_b, L0_gnn_gru_wih, L0_gnn_gru_whh, L0_gnn_gru_bih, L0_gnn_gru_bhh, L0_gnn_out_w, L0_gnn_out_b), axis=-1)
    x = _layernorm(x + _L1_gnn_ref(x, edge_index, edge_type_8, L1_gnn_W1, L1_gnn_root1, L1_gnn_b1, L1_gnn_W2, L1_gnn_root2, L1_gnn_b2, L1_gnn_W3, L1_gnn_root3, L1_gnn_b3, L1_gnn_res_w, L1_gnn_res_b), axis=-1)
    x = _layernorm(x + _L2_gnn_ref(x, edge_index, L2_gnn_W, L2_gnn_b), axis=-1)
    x = _layernorm(x + _L3_gnn_ref(x, edge_index, edge_attr_16, L3_gnn_W1, L3_gnn_b1, L3_gnn_W2, L3_gnn_b2), axis=-1)
    return x

_drawn_inputs = setup_inputs


def setup_inputs(seed=0):
    import zlib

    import numpy as np

    out = dict(_drawn_inputs(seed))
    spreads = {'L0_gnn_out_b': (0.0, 0.1),
     'L1_gnn_b1': (0.0, 0.1),
     'L1_gnn_b2': (0.0, 0.1),
     'L1_gnn_b3': (0.0, 0.465),
     'L1_gnn_res_b': (0.0, 0.1)}
    factors = {'L0_gnn_node_proj_b': 4.268,
     'L0_gnn_gru_bih': 3.848,
     'L0_gnn_gru_bhh': 5.863,
     'L2_gnn_b': 6.698,
     'L3_gnn_b1': 8.0,
     'L3_gnn_b2': 6.322}
    for name, (base, spread) in spreads.items():
        noise = np.random.default_rng([zlib.crc32(name.encode()), seed]).standard_normal(out[name].shape)
        drawn = base * np.exp(spread * noise) if base else spread * noise
        out[name] = jnp.asarray(drawn.astype(out[name].dtype))
    for name, factor in factors.items():
        out[name] = (out[name] * factor).astype(out[name].dtype)
    return out
```

```python
from contextlib import ExitStack

import numpy as np
import concourse.bass as bass
from concourse import mybir

F32 = mybir.dt.float32
I32 = mybir.dt.int32
ALU = mybir.AluOpType
ACT = mybir.ActivationFunctionType
AX = mybir.AxisListType
ds = bass.ds

P = 128
NODES = 3125
EDGES = 53125
NB = 26
NP = NB * P
CH = 416
NCH = NP // CH
T = 8
A = 16
TC = T + A
G = 8
GE = G * P
NG = -(-EDGES // GE)
NT = NG * G
SUB = 4
PASSES = NG // SUB
NONE = 8191
HT = 16
HW = HT * NB
HPAIRS = NT // (2 * HT)
MV = NB * A + NB
ST = 448
SPASSES = ST // (SUB * G)
EPS = 1e-5
assert NG % SUB == 0 and NP % (2 * CH) == 0 and NODES + P <= NP and MV <= 512 and HW <= 512
assert ST % (SUB * G) == 0 and ST * P >= EDGES + NB * (P - 1) and NT % (2 * HT) == 0

W_NAMES = (["proj"] + [f"edge{l}_{t}" for l in range(2) for t in range(T)]
           + [f"{s}{l}_{g}" for l in range(2) for s in ("wih", "whh") for g in "rzn"] + ["out", "res"]
           + [f"rel{l}_{t}" for l in range(3) for t in range(T)] + [f"root{l}" for l in range(3)]
           + ["gcn", "w1x", "w1a", "w2", "ident", "center", "mean", "before", "ones", "dst_count"])
W_AT = {n: i * P for i, n in enumerate(W_NAMES)}
B_NAMES = (["proj"] + [f"{s}{l}_{g}" for l in range(2) for s in ("bih", "bhh") for g in "rzn"]
           + [f"both{l}_{g}" for l in range(2) for g in "rz"]
           + ["out", "res", "b0", "b1", "b2", "gcn", "mlp1", "mlp2", "eps"])
B_AT = {n: i for i, n in enumerate(B_NAMES)}
INV_ROWS, DST_ROWS, SRC_ROWS = slice(0, T), slice(32, 32 + TC), slice(64, 64 + A)


class Steps:

    def __init__(self, eng, sem):
        self.eng, self.sem, self.base, self.j = eng, sem, 0, 0

    def did(self, ins):
        ins.then_inc(self.sem, 1)
        self.j += 1

    def settle(self):
        self.eng.wait_ge(self.sem, self.base + self.j)

    def do(self, ins):
        self.did(ins)
        self.settle()

    def enter(self, it, step):
        self.start, self.step, self.base, self.j = self.base + self.j, step, self.base + self.j + it * step, 0

    def leave(self, passes):
        assert self.j == self.step, self.j
        self.base, self.j = self.start + passes * self.step, 0


TOTALS = {
    "tab_staged": NB, "tab_mm": NB + 2, "tab_act": NB + 2, "tab_dve": NB + 2, "table_stored": 16 * (NB // 2),
    "summed": SUB + NG, "onehot": NG, "added": 1 + NG, "gathered": 16 * G * PASSES, "hidden": 1,
    "marked": NG, "mark_loaded": 16 * PASSES, "zeros": 1, "opened": 1, "extra_ready": SUB + NG, "extra_used": 2 + NG,
    "gru_used": 2 + NCH, "gru_mm": NCH, "gru_rz": NCH, "gru_cand": NCH, "gru_n": NCH, "gru_mixed": 1 + NCH, "gru_h": 1 + NCH,
    "ln_in": 1, "ln_free": 2 + NCH, "ln_center": NCH, "ln_sq": NCH, "ln_var": NCH, "ln_sd": NCH, "ln_out": NCH,
}
FIRST_RUN = {"zeros": 2, "opened": 2, "extra_ready": 2, "extra_used": 2, "hidden": 2}


def graph_kernel(nc, xT_d, dst_rows_d, dst_d, src_d, typ_d, mark_d, w_d, b_d, iota_d, out_d):
    with ExitStack() as ctx:
        def sb(name, shape, dt=F32):
            return ctx.enter_context(nc.sbuf_tensor(name, shape, dt))

        sems = {}

        def q(name):
            if name not in sems:
                sems[name] = ctx.enter_context(nc.semaphore(name))
            return sems[name]

        def after(eng, name, run, count):
            kind = name.rsplit("_", 1)[0] if name[-1].isdigit() else name
            eng.wait_ge(q(name), TOTALS[kind] * (run - FIRST_RUN.get(kind, 0)) + count)

        table_d = nc.dram_tensor("messages", (NP, T * P), F32).ap()
        gcn_table_d = nc.dram_tensor("gcn_rows", (NP, P), F32).ap()
        table_rows = table_d.rearrange("n (t d) -> (n t) d", t=T)

        ps = ctx.enter_context(nc.psum_tensor("ps", [P, 8, 512], F32))
        psf = ps[:].rearrange("p a b -> p (a b)")

        w = sb("w", [P, len(W_NAMES) * P])
        bias = sb("bias", [P, len(B_NAMES)])
        iota = sb("iota", [P, 512])
        x = sb("x", [P, NP])
        h = sb("h", [P, NP])
        acc = sb("acc", [P, NP])
        res = sb("res", [P, NP])
        nodes = sb("nodes", [P, NP])
        dst = sb("dst", [P, NT], I32)
        src = sb("src", [P, NT], I32)
        typ = sb("typ", [P, NT], I32)
        row_idx = sb("row_idx", [P, NT], I32)
        dst_lo = sb("dst_lo", [P, NT])
        src_lo = sb("src_lo", [P, NT])
        src_hi = sb("src_hi", [P, NT])
        typ_f = sb("typ_f", [P, NT])
        edge_w = sb("edge_w", [P, NT])
        base_f = sb("base_f", [P, NG])
        base_i = sb("base_i", [P, NG], I32)
        base_diag = sb("base_diag", [NG, NG])
        first = sb("first", [NG, 1])
        msg = sb("msg", [P, SUB, G, P])
        mark = sb("mark", [P, SUB, G * TC])
        idx_buf = sb("idx_buf", [P, SUB, G], I32)
        onehot = sb("onehot", [P, 2, G, P])
        lane1h = sb("lane1h", [P, 2, G, P])
        big = sb("big", [P, 2, G * ST])
        gcn_idx = sb("gcn_idx", [P, ST], I32)
        gcn_lo = sb("gcn_lo", [P, ST])
        gcn_base = sb("gcn_base", [P, ST], I32)
        slot = sb("slot", [P, NT])
        slot_i = typ
        slot_lane = sb("slot_lane", [P, NT])
        slot_tile = sb("slot_tile", [P, NT])
        payload = sb("payload", [P, NT])
        valid = slot_lane
        totals = lane1h[0:NB, 1, :, :].rearrange("p a b -> p (a b)")[:, 0:NT]
        scanned = lane1h[0:NB, 1, :, :].rearrange("p a b -> p (a b)")[:, 512:512 + NT]
        blk = sb("blk", [NB, 8])
        blk_i = sb("blk_i", [NB, 2], I32)
        by_src = sb("by_src", [P, MV])
        deg = sb("deg", [P, 4, NB])
        dinv = sb("dinv", [P, NB])
        tmp = sb("tmp", [P, 8, CH])
        flat = big[:].rearrange("p a b -> p (a b)")
        scratch_i = flat[:, 0:ST].bitcast(I32)

        def wt(name, n=1):
            return w[:, W_AT[name]:W_AT[name] + n * P]

        def bs(name):
            return bias[:, B_AT[name]:B_AT[name] + 1]

        def chunk(buf, c):
            return buf[:, ds(c * CH, CH)]

        loops = [
            (row_idx, dst_lo, False, table_rows, PASSES, "count"),
            (row_idx, dst_lo, False, table_rows, PASSES, "weigh"),
            (row_idx, dst_lo, True, table_rows, PASSES, "attr_by_src"),
            (row_idx, dst_lo, True, table_rows, PASSES, "scatter"),
            (row_idx, dst_lo, True, table_rows, PASSES, None),
            (gcn_idx, gcn_lo, False, gcn_table_d, SPASSES, None),
        ]
        mark_free = {0: "count_mm", 1: "turned", 2: "extra_ready"}
        FLUSH = 5

        block = ctx.enter_context(nc.Block())

        @block.sync
        def _(eng):
            eng.dma_start(flat[0:NG, 0:GE].bitcast(I32), dst_rows_d).then_inc(q("loaded"), 16)
            for buf, d in ((dst, dst_d), (src, src_d), (typ, typ_d), (bias, b_d), (iota, iota_d)):
                eng.dma_start(buf[:], d).then_inc(q("loaded"), 16)
            eng.dma_start(w[:], w_d).then_inc(q("loaded_w"), 16)
            eng.dma_start(x[:], xT_d).then_inc(q("loaded_w"), 16)

            for k in range(5):
                with eng.Fori(0, NB // 2) as it:
                    for p in range(2):
                        after(eng, "tab_act", k, it * 2 + p + 3)
                        after(eng, "tab_dve", k, it * 2 + p + 3)
                        eng.dma_start(table_d[ds((it * 2 + p) * P, P), :], flat[:, p * 1024:p * 1024 + 1024])\
                           .then_inc(q(f"table_stored_{p}"), 16)
                if k in mark_free:
                    with eng.Fori(0, PASSES) as it:
                        for s in range(SUB):
                            eng.wait_ge(q(mark_free[k]), it * SUB + s + 1)
                            eng.dma_start(mark[:, s, :], mark_d[:, ds((it * SUB + s) * (G * TC), G * TC)])\
                               .then_inc(q(f"mark_loaded_{s}"), 16)
            eng.wait_ge(q("gcn_rows"), NB + 2)
            eng.dma_start(gcn_table_d.rearrange("(b p) d -> p b d", p=P),
                          flat[:, 0:NB * P].rearrange("p (b d) -> p b d", b=NB)).then_inc(q("gcn_stored"), 16)
            after(eng, "ln_out", 3, NCH)
            eng.dma_start(out_d, x[:]).then_inc(q("out_stored"), 16)
            eng.wait_ge(q("out_stored"), 16)

        @block.gpsimd
        def _(eng):
            st = Steps(eng, q("pool_steps"))

            def stage_blocks(k, source):
                with eng.Fori(0, NB // 2) as it:
                    for p in range(2):
                        after(eng, "tab_mm", k, it * 2 + p + 1)
                        eng.tensor_copy(lane1h[:, 0, p, :], source[:, ds((it * 2 + p) * P, P)])\
                           .then_inc(q("tab_staged"), 1)

            def gather(k):
                idx, lo, weighted, table, passes, extra = loops[k]
                with eng.Fori(0, passes) as it:
                    st.enter(it, SUB)
                    for s in range(SUB):
                        after(eng, "summed", k, it * SUB + s + 1)
                        st.do(eng.tensor_copy(idx_buf[:, s, :], idx[:, ds((it * SUB + s) * G, G)]))
                        eng.sem_inc(q("rows_known"), 1)
                        for t in range(G):
                            eng.indirect_dma_start(msg[:, s, t, :], None, table,
                                                   bass.IndirectOffsetOnAxis(ap=idx_buf[:, s, t:t + 1], axis=0))\
                               .then_inc(q(f"gathered_{s}"), 16)
                    st.leave(passes)

            eng.wait_ge(q("rows_ready"), 1)
            for k in range(5):
                if k == 0:
                    eng.wait_ge(q("proj_used"), 2 + NCH)
                elif k == 1:
                    after(eng, "gru_h", 0, 1 + NCH)
                elif k == 2:
                    after(eng, "ln_out", 0, NCH)
                else:
                    after(eng, "hidden", k - 1, 1)
                stage_blocks(k, x if k == 2 else h)
                for p in range(2):
                    after(eng, f"table_stored_{p}", k, 16 * (NB // 2))
                gather(k)
            after(eng, "ln_out", 1, NCH)
            stage_blocks(FLUSH, x)
            eng.wait_ge(q("gcn_stored"), 16)
            gather(FLUSH)

        @block.tensor
        def _(eng):
            mm = eng.matmul

            def chunks(name, weight, source):
                with eng.Fori(0, NCH // 2) as it:
                    for p in range(2):
                        eng.wait_ge(q(f"{name}_used"), it * 2 + p + 1)
                        mm(ps[:, 4 + p, 0:CH], wt(weight), chunk(source, it * 2 + p), start=True, stop=True)\
                            .then_inc(q(f"{name}_mm"), 1)

            def table(k, weight):
                eng.sem_inc(q("tab_mm"), 2)
                with eng.Fori(0, NB // 2) as it:
                    for p in range(2):
                        after(eng, "tab_staged", k, it * 2 + p + 1)
                        after(eng, "tab_act", k, it * 2 + p + 1)
                        after(eng, "tab_dve", k, it * 2 + p + 1)
                        rhs = wt(weight, T)
                        mm(ps[:, 2 * p, :], lane1h[:, 0, p, :], rhs[:, 0:512], start=True, stop=True)
                        mm(ps[:, 2 * p + 1, :], lane1h[:, 0, p, :], rhs[:, 512:1024], start=True, stop=True)\
                            .then_inc(q("tab_mm"), 1)

            def edge_sums(k):
                idx, lo, weighted, tab, passes, extra = loops[k]
                big_product = extra in ("attr_by_src", "scatter")
                n = MV if extra == "attr_by_src" else ST
                eng.sem_inc(q("summed"), SUB)
                if extra == "count":
                    eng.sem_inc(q("count_mm"), SUB)
                if extra == "weigh":
                    eng.sem_inc(q("turned"), SUB)
                    eng.sem_inc(q("weigh_mm"), 1)
                    eng.wait_ge(q("inv_ready"), 1)
                if big_product:
                    after(eng, "zeros", k, 1)
                    mm(ps[:, 7, 0:n], wt("ones"), flat[:, G * ST:G * ST + n], start=True, stop=False,
                       skip_group_check=True).then_inc(q("opened"), 1)
                    eng.sem_inc(q("extra_used"), 2)
                with eng.Fori(0, passes) as it:
                    for s in range(SUB):
                        g = it * SUB + s
                        if extra == "weigh":
                            base = eng.value_load(base_i[0:1, ds(g, 1)], min_val=0, max_val=NP - P)
                        after(eng, "onehot", k, g + 1)
                        after(eng, f"gathered_{s}", k, (it + 1) * (16 * G))
                        for t in range(G):
                            if k == FLUSH:
                                out = ps[:, 2 * (s % 2) + t // 4, (t % 4) * P:(t % 4) * P + P]
                                last = mm(out, msg[:, s, t, :], onehot[:, s % 2, t, :], start=True, stop=True)
                            else:
                                last = mm(ps[:, s % 2, 0:P], msg[:, s, t, :], onehot[:, s % 2, t, :],
                                          start=t == 0, stop=t == G - 1)
                        last.then_inc(q("summed"), 1)
                        if extra == "count":
                            after(eng, "marked", 0, g + 1)
                            for t in range(G):
                                last = mm(ps[DST_ROWS, 2, 0:P], mark[:, s, t * TC:(t + 1) * TC],
                                          onehot[:, s % 2, t, :], start=t == 0, stop=t == G - 1)
                            last.then_inc(q("count_mm"), 1)
                        if extra == "weigh":
                            after(eng, "marked", 1, g + 1)
                            for t in range(G):
                                last = mm(ps[0:T, 2 + t // 4, (t % 4) * P:(t % 4) * P + P],
                                          mark[:, s, t * TC:t * TC + T], wt("ident"), start=True, stop=True)
                            last.then_inc(q("turned"), 1)
                            eng.wait_ge(q("turned_copied"), g + 1)
                            for t in range(G):
                                last = mm(ps[:, 4 + t // 4, (t % 4) * P:(t % 4) * P + P],
                                          flat[INV_ROWS, t * P:(t + 1) * P], nodes[INV_ROWS, ds(base, P)],
                                          start=True, stop=True)
                            last.then_inc(q("weigh_mm"), 1)
                        if big_product:
                            after(eng, "extra_ready", k, g + 1 + SUB * (k == 2))
                            for t in range(G):
                                last = mm(ps[:, 7, 0:n], lane1h[:, s % 2, t, :], big[:, s % 2, t * ST:t * ST + n],
                                          start=False, stop=False, skip_group_check=True)
                            last.then_inc(q("extra_used"), 1)

            def gru(l):
                with eng.Fori(0, NCH // 2) as it:
                    for p in range(2):
                        c = it * 2 + p
                        after(eng, "gru_used", l, c + 1)
                        for i, (a, b) in enumerate((("wih", "r"), ("wih", "z"), ("wih", "n"), ("whh", "n"))):
                            last = mm(ps[:, 4 * p + i, 0:CH], wt(f"{a}{l}_{b}"), chunk(acc if a == "wih" else h, c),
                                      start=True, stop=i >= 2)
                            if i < 2:
                                last = mm(ps[:, 4 * p + i, 0:CH], wt(f"whh{l}_{b}"), chunk(h, c),
                                          start=False, stop=True)
                        last.then_inc(q("gru_mm"), 1)

            def norm(n):
                after(eng, "ln_in", n, 1)
                with eng.Fori(0, NCH // 2) as it:
                    for p in range(2):
                        c = it * 2 + p
                        after(eng, "ln_free", n, c + 1)
                        mm(ps[:, p, 0:CH], wt("center"), chunk(acc, c), start=True, stop=True)\
                            .then_inc(q("ln_center"), 1)
                        after(eng, "ln_sq", n, c + 1)
                        mm(ps[:, 2 + p, 0:CH], wt("mean"), tmp[:, p, :], start=True, stop=True)\
                            .then_inc(q("ln_var"), 1)

            def rank():
                with eng.Fori(0, HPAIRS) as it:
                    for p in range(2):
                        eng.wait_ge(q("rank_h"), it * 2 + p + 1)
                        for j in range(HT):
                            mm(ps[0:NB, 2 + p, j:j + 1], big[:, p, j * NB:(j + 1) * NB], wt("ones")[:, 0:1],
                               start=True, stop=True)
                        mm(ps[:, p, 0:HW], wt("before"), big[:, p, 0:HW], start=True, stop=True)\
                            .then_inc(q("rank_mm"), 1)
                eng.wait_ge(q("block_size"), 1)
                mm(ps[0:NB, 4, 0:1], w[0:NB, W_AT["before"]:W_AT["before"] + NB], blk[:, 1:2], start=True, stop=True)\
                    .then_inc(q("block_start"), 1)
                eng.wait_ge(q("block_ended"), 1)
                mm(ps[:, 5, 0:ST], w[0:NB, W_AT["ones"]:W_AT["ones"] + P], flat[0:NB, 0:ST], start=True, stop=True)\
                    .then_inc(q("tile_block"), 1)
                with eng.Fori(0, HPAIRS) as it:
                    for p in range(2):
                        eng.wait_ge(q("rank_diag"), it * 2 + p + 1)
                        mm(ps[:, p, 0:HW], w[0:NB, W_AT["ones"]:W_AT["ones"] + P], big[0:NB, p, HW:2 * HW],
                           start=True, stop=True).then_inc(q("rank_base"), 1)

            eng.wait_ge(q("loaded_w"), 32)
            eng.wait_ge(q("diag_ready"), 1)
            mm(ps[:, 7, 0:NG], w[0:NG, W_AT["ones"]:W_AT["ones"] + P], base_diag[:], start=True, stop=True)\
                .then_inc(q("base_mm"), 1)
            chunks("proj", "proj", x)
            for l in range(2):
                table(l, f"edge{l}_0")
                edge_sums(l)
                after(eng, "added", l, 1 + NG)
                if l == 0:
                    eng.wait_ge(q("counted"), 1 + NG)
                else:
                    eng.wait_ge(q("weighed"), NG)
                gru(l)
            after(eng, "gru_h", 1, 1 + NCH)
            chunks("out", "out", h)
            norm(0)
            after(eng, "ln_out", 0, NCH)
            chunks("res", "res", x)
            for k in range(2, 5):
                table(k, f"rel{k - 2}_0")
                chunks(f"root{k}", f"root{k - 2}", x if k == 2 else h)
                eng.wait_ge(q(f"root{k}_used"), 2 + NCH)
                if k == 3:
                    rank()
                edge_sums(k)
            norm(1)
            eng.sem_inc(q("tab_mm"), 2)
            with eng.Fori(0, NB // 2) as it:
                for p in range(2):
                    after(eng, "tab_staged", 5, it * 2 + p + 1)
                    eng.wait_ge(q("gcn_rows"), it * 2 + p + 1)
                    mm(ps[:, p, 0:P], lane1h[:, 0, p, :], wt("gcn"), start=True, stop=True).then_inc(q("tab_mm"), 1)
            edge_sums(FLUSH)
            after(eng, "added", FLUSH, 1 + ST)
            for b in range(NB):
                last = mm(psf[:, b * P:(b + 1) * P], dinv[:, b:b + 1].to_broadcast([P, P]), wt("ident"),
                          start=True, stop=True)
            last.then_inc(q("dinv_mm"), 1)
            norm(2)
            after(eng, "ln_out", 2, NCH)
            for b in range(NB):
                last = mm(psf[SRC_ROWS, b * P:(b + 1) * P], by_src[:, b * A:(b + 1) * A], wt("ident"),
                          start=True, stop=True)
            last.then_inc(q("src_turned"), 1)
            eng.wait_ge(q("src_copied"), 1)
            for c in range(NCH):
                last = mm(ps[:, c, 0:CH], wt("dst_count"), nodes[:, c * CH:(c + 1) * CH], start=True, stop=True)
            last.then_inc(q("dst_count_mm"), 1)
            eng.wait_ge(q("nodes_ready"), 1)
            with eng.Fori(0, NCH // 2) as it:
                for p in range(2):
                    c = it * 2 + p
                    eng.wait_ge(q("mlp_used"), c + 1)
                    mm(ps[:, p, 0:CH], wt("w1x"), chunk(x, c), start=True, stop=False)
                    mm(ps[:, p, 0:CH], wt("w1a"), chunk(nodes, c), start=False, stop=True).then_inc(q("mlp1_mm"), 1)
                    eng.wait_ge(q("mlp_hidden"), c + 1)
                    mm(ps[:, 2 + p, 0:CH], wt("w2"), tmp[:, 2 + p, :], start=True, stop=True).then_inc(q("mlp2_mm"), 1)
            norm(3)

        @block.scalar
        def _(eng):
            act = nc.scalar.activation
            st = Steps(eng, q("act_steps"))

            def chunks(name, out, func, b):
                eng.sem_inc(q(f"{name}_used"), 2)
                with eng.Fori(0, NCH // 2) as it:
                    for p in range(2):
                        c = it * 2 + p
                        eng.wait_ge(q(f"{name}_mm"), c + 1)
                        act(chunk(out, c), ps[:, 4 + p, 0:CH], func, bias=bs(b)).then_inc(q(f"{name}_used"), 1)

            def table(k):
                eng.sem_inc(q("tab_act"), 2)

                def pair(it):
                    for p in range(2):
                        after(eng, "tab_mm", k, it * 2 + p + 3)
                        if not isinstance(it, int):
                            after(eng, f"table_stored_{p}", k, it * 16)
                        act(flat[:, p * 1024:p * 1024 + 512], ps[:, 2 * p, :], ACT.Copy).then_inc(q("tab_act"), 1)

                pair(0)
                with eng.Fori(1, NB // 2) as it:
                    pair(it)

            def gru(l):
                eng.sem_inc(q("gru_used"), 2)
                eng.sem_inc(q("gru_h"), 1)
                with eng.Fori(0, NCH // 2) as it:
                    for p in range(2):
                        c = it * 2 + p
                        after(eng, "gru_mm", l, c + 1)
                        after(eng, "gru_mixed", l, c + 1)
                        act(tmp[:, 0, :], ps[:, 4 * p, 0:CH], ACT.Sigmoid, bias=bs(f"both{l}_r"))
                        act(tmp[:, 1, :], ps[:, 4 * p + 1, 0:CH], ACT.Sigmoid, bias=bs(f"both{l}_z"))\
                            .then_inc(q("gru_rz"), 1)
                        after(eng, "gru_cand", l, c + 1)
                        act(tmp[:, 3, :], tmp[:, 2, :], ACT.Tanh, bias=bs(f"bih{l}_n")).then_inc(q("gru_n"), 1)
                        eng.sem_inc(q("gru_used"), 1)
                        after(eng, "gru_mixed", l, c + 2)
                        act(chunk(h, c), tmp[:, 5, :], ACT.Relu).then_inc(q("gru_h"), 1)

            def norm(n):
                with eng.Fori(0, NCH // 2) as it:
                    for p in range(2):
                        c = it * 2 + p
                        after(eng, "ln_center", n, c + 1)
                        act(tmp[:, p, :], ps[:, p, 0:CH], ACT.Square).then_inc(q("ln_sq"), 1)
                        after(eng, "ln_var", n, c + 1)
                        act(tmp[:, 2 + p, :], ps[:, 2 + p, 0:CH], ACT.Sqrt, bias=bs("eps")).then_inc(q("ln_sd"), 1)

            eng.wait_ge(q("bias_ready"), 1)
            chunks("proj", h, ACT.Relu, "proj")
            for l in range(2):
                table(l)
                if l == 1:
                    for p in range(2):
                        after(eng, f"table_stored_{p}", l, 16 * (NB // 2))
                    with eng.Fori(0, PASSES) as it:
                        for s in range(SUB):
                            g = it * SUB + s
                            eng.wait_ge(q("turned"), g + 1 + SUB)
                            eng.wait_ge(q("weigh_mm"), g + 1)
                            act(flat[0:T, 0:GE], psf[0:T, 1024:1024 + GE], ACT.Copy).then_inc(q("turned_copied"), 1)
                gru(l)
            norm(0)
            chunks("res", res, ACT.Identity, "res")
            for k in range(2, 5):
                table(k)
                if k >= 3:
                    after(eng, "hidden", k - 1, 1)
                chunks(f"root{k}", acc, ACT.Identity, f"b{k - 2}")
                if k == 2:
                    eng.wait_ge(q("deg1"), 1)
                    act(deg[:, 1, :], deg[:, 0, :], ACT.Sqrt).then_inc(q("deg_sqrt"), 1)
            norm(1)
            eng.sem_inc(q("gcn_rows"), 2)
            with eng.Fori(0, NB // 2) as it:
                for p in range(2):
                    after(eng, "tab_mm", 5, it * 2 + p + 3)
                    act(flat[:, ds((it * 2 + p) * P, P)], ps[:, p, 0:P], ACT.Copy, scale=dinv[:, ds(it * 2 + p, 1)])\
                        .then_inc(q("gcn_rows"), 1)
            norm(2)
            eng.wait_ge(q("src_turned"), 1)
            act(nodes[SRC_ROWS, :], psf[SRC_ROWS, 0:NP], ACT.Copy).then_inc(q("src_copied"), 1)
            eng.sem_inc(q("mlp_used"), 2)
            with eng.Fori(0, NCH // 2) as it:
                for p in range(2):
                    c = it * 2 + p
                    eng.wait_ge(q("mlp1_mm"), c + 1)
                    act(tmp[:, p, :], ps[:, p, 0:CH], ACT.Identity, bias=bs("mlp1")).then_inc(q("mlp_pre"), 1)
            norm(3)

        @block.vector
        def _(eng):
            vec = nc.vector
            st = Steps(eng, q("dve_steps"))

            def over_tiles(buf, n):
                return buf.unsqueeze(2).to_broadcast([buf.shape[0], buf.shape[1], n])

            def over_lanes(row, n, parts=P):
                return row.unsqueeze(1).to_broadcast([parts, n, row.shape[1]])

            def prep():
                eng.wait_ge(q("loaded"), 6 * 16)
                eng.wait_ge(q("loaded_w"), 32)
                st.do(vec.tensor_reduce(first[:], flat[0:NG, 0:GE].bitcast(I32), AX.X, ALU.min))
                vec.tensor_scalar(base_diag[:], w[0:NG, W_AT["ident"]:W_AT["ident"] + NG], first[:], None, ALU.mult)\
                   .then_inc(q("diag_ready"), 1)
                for l in range(2):
                    for g in "rz":
                        st.did(vec.tensor_tensor(bs(f"both{l}_{g}"), bs(f"bih{l}_{g}"), bs(f"bhh{l}_{g}"), ALU.add))
                st.settle()
                vec.engine_nop().then_inc(q("bias_ready"), 1)
                st.did(vec.memset(nodes[:], 0.0))
                st.did(vec.tensor_scalar(valid[:], src[:], float(NONE), None, ALU.is_lt))
                st.did(vec.tensor_copy(typ_f[:], typ[:]))
                st.settle()
                st.do(vec.tensor_scalar(slot_i[:], src[:], P - 1, None, ALU.bitwise_and))
                st.did(vec.tensor_copy(src_lo[:], slot_i[:]))
                st.do(vec.scalar_tensor_tensor(out=slot[:], in0=src[:], scalar=float(T), in1=typ_f[:],
                                               op0=ALU.mult, op1=ALU.add))
                st.did(vec.tensor_tensor(row_idx[:], slot[:], valid[:], ALU.mult))
                st.do(vec.tensor_scalar(slot_i[:], src[:], 7, None, ALU.arith_shift_right))
                st.did(vec.tensor_copy(src_hi[:], slot_i[:]))
                st.do(vec.tensor_scalar(payload[:], src_lo[:], 1.0, 4096.0, ALU.add, ALU.mult))
                st.do(vec.tensor_tensor(payload[:], payload[:], dst[:], ALU.add))
                st.do(vec.tensor_tensor(payload[:], payload[:], valid[:], ALU.mult))
                eng.wait_ge(q("base_mm"), 1)
                st.did(vec.tensor_copy(base_f[:], ps[:, 7, 0:NG]))
                st.did(vec.tensor_copy(base_i[:], ps[:, 7, 0:NG]))
                st.settle()
                st.do(vec.tensor_tensor(dst_lo[:].rearrange("p (g k) -> p g k", k=G),
                                        dst[:].rearrange("p (g k) -> p g k", k=G), over_tiles(base_f[:], G),
                                        ALU.subtract))
                vec.engine_nop().then_inc(q("rows_ready"), 1)

            def table(k):
                eng.sem_inc(q("tab_dve"), 2)

                def pair(it):
                    for p in range(2):
                        after(eng, "tab_mm", k, it * 2 + p + 3)
                        if not isinstance(it, int):
                            after(eng, f"table_stored_{p}", k, it * 16)
                        vec.tensor_copy(flat[:, p * 1024 + 512:p * 1024 + 1024], ps[:, 2 * p + 1, :])\
                           .then_inc(q("tab_dve"), 1)

                pair(0)
                with eng.Fori(1, NB // 2) as it:
                    pair(it)

            def edge_sums(k):
                idx, lo, weighted, tab, passes, extra = loops[k]
                lane = {"attr_by_src": src_lo, "scatter": slot_lane}.get(extra)
                if k in (0, 1, FLUSH):
                    st.do(vec.memset(acc[:], 0.0))
                else:
                    eng.wait_ge(q(f"root{k}_used"), 2 + NCH)
                if k < FLUSH:
                    for p in range(2):
                        after(eng, f"table_stored_{p}", k, 16 * (NB // 2))
                if lane is not None:
                    vec.memset(flat[:, G * ST:G * ST + 512], 0.0).then_inc(q("zeros"), 1)
                    after(eng, "opened", k, 1)
                if k == 2:
                    eng.sem_inc(q("extra_ready"), SUB)
                eng.sem_inc(q("added"), 1)
                if extra == "count":
                    eng.sem_inc(q("counted"), 1)
                with eng.Fori(0, passes) as it:
                    st.enter(it, {"weigh": SUB, "attr_by_src": 3 * SUB - SUB, "scatter": 0}.get(extra, 0))
                    for s in range(SUB):
                        g = it * SUB + s
                        if k != FLUSH:
                            base = eng.value_load(base_i[0:1, ds(g, 1)], min_val=0, max_val=NP - P)
                        if weighted:
                            for t in range(G):
                                last = vec.tensor_scalar(onehot[:, s % 2, t, :], iota[:, 0:P], lo[:, ds(g * G + t, 1)],
                                                         edge_w[:, ds(g * G + t, 1)], ALU.is_equal, ALU.mult)
                        else:
                            last = vec.tensor_tensor(onehot[:, s % 2, :, :], over_lanes(iota[:, 0:P], G),
                                                     over_tiles(lo[:, ds(g * G, G)], P), ALU.is_equal)
                        last.then_inc(q("onehot"), 1)
                        if k in (0, 1):
                            after(eng, f"mark_loaded_{s}", k, (it + 1) * 16)
                            vec.tensor_tensor(mark[:, s, :].rearrange("p (k c) -> p k c", c=TC)[:, :, 0:T],
                                              over_tiles(typ_f[:, ds(g * G, G)], T), over_lanes(iota[:, 0:T], G),
                                              ALU.is_equal).then_inc(q("marked"), 1)
                        if lane is not None:
                            after(eng, "extra_used", k, g + 1)
                            if k == 2:
                                st.did(vec.tensor_tensor(lane1h[:, s % 2, :, :], over_lanes(iota[:, 0:P], G),
                                                         over_tiles(lane[:, ds(g * G, G)], P), ALU.is_equal))
                                cols = big[:, s % 2, :].rearrange("p (k c) -> p k c", c=ST)
                                hi1h = cols[:, :, NB * A:MV]
                                st.do(vec.tensor_tensor(hi1h, over_lanes(iota[:, 0:NB], G),
                                                        over_tiles(src_hi[:, ds(g * G, G)], NB), ALU.is_equal))
                                attrs = mark[:, s, :].rearrange("p (k c) -> p k c", c=TC)[:, :, T:TC]
                                after(eng, f"mark_loaded_{s}", k, (it + 1) * 16)
                                vec.tensor_tensor(cols[:, :, 0:NB * A].rearrange("p k (b a) -> p k b a", a=A),
                                                  hi1h.unsqueeze(3).to_broadcast([P, G, NB, A]),
                                                  attrs.unsqueeze(2).to_broadcast([P, G, NB, A]),
                                                  ALU.mult).then_inc(q("extra_ready"), 1)
                            else:
                                vec.tensor_tensor(lane1h[:, s % 2, :, :], over_lanes(iota[:, 0:P], G),
                                                  over_tiles(lane[:, ds(g * G, G)], P), ALU.is_equal)
                                for t in range(G):
                                    last = vec.tensor_scalar(big[:, s % 2, t * ST:(t + 1) * ST], iota[:, 0:ST],
                                                             slot_tile[:, ds(g * G + t, 1)],
                                                             payload[:, ds(g * G + t, 1)], ALU.is_equal, ALU.mult)
                                last.then_inc(q("extra_ready"), 1)
                        after(eng, "summed", k, g + 1 + SUB)
                        if k == FLUSH:
                            for t in range(G):
                                base = eng.value_load(gcn_base[0:1, ds(g * G + t, 1)], min_val=0, max_val=NP - P)
                                after(eng, "added", k, g * G + t + 1)
                                vec.tensor_tensor(acc[:, ds(base, P)], acc[:, ds(base, P)],
                                                  ps[:, 2 * (s % 2) + t // 4, (t % 4) * P:(t % 4) * P + P],
                                                  ALU.add).then_inc(q("added"), 1)
                        else:
                            after(eng, "added", k, g + 1)
                            vec.tensor_tensor(acc[:, ds(base, P)], acc[:, ds(base, P)], ps[:, s % 2, 0:P],
                                              ALU.add).then_inc(q("added"), 1)
                        if extra == "count":
                            eng.wait_ge(q("count_mm"), g + 1 + SUB)
                            eng.wait_ge(q("counted"), g + 1)
                            vec.tensor_tensor(nodes[DST_ROWS, ds(base, P)], nodes[DST_ROWS, ds(base, P)],
                                              ps[DST_ROWS, 2, 0:P], ALU.add).then_inc(q("counted"), 1)
                        if extra == "weigh":
                            eng.wait_ge(q("weigh_mm"), g + 2)
                            prod = flat[:, G * ST:G * ST + GE].rearrange("p (k c) -> p k c", c=P)
                            st.do(vec.tensor_tensor(prod, onehot[:, s % 2, :, :],
                                                    psf[:, 2048:2048 + GE].rearrange("p (k c) -> p k c", c=P), ALU.mult))
                            vec.tensor_reduce(edge_w[:, ds(g * G, G)], prod, AX.X, ALU.add).then_inc(q("weighed"), 1)
                            eng.wait_ge(q("weighed"), g + 1)
                    st.leave(passes)
                after(eng, "added", k, 1 + passes * SUB * (G if k == FLUSH else 1))
                if extra == "count":
                    eng.wait_ge(q("counted"), 1 + NG)
                    st.do(vec.tensor_scalar(nodes[INV_ROWS, :], nodes[32:32 + T, :], 1.0, None, ALU.max))
                    vec.reciprocal(nodes[INV_ROWS, :], nodes[INV_ROWS, :]).then_inc(q("inv_ready"), 1)

            def gru(l):
                eng.sem_inc(q("gru_mixed"), 1)
                with eng.Fori(0, NCH // 2) as it:
                    st.enter(it, 8)
                    for p in range(2):
                        c = it * 2 + p
                        after(eng, "gru_rz", l, c + 1)
                        st.do(vec.scalar_tensor_tensor(out=tmp[:, 4, :], in0=ps[:, 4 * p + 3, 0:CH],
                                                       scalar=bs(f"bhh{l}_n"), in1=tmp[:, 0, :], op0=ALU.add, op1=ALU.mult))
                        vec.tensor_tensor(tmp[:, 2, :], tmp[:, 4, :], ps[:, 4 * p + 2, 0:CH], ALU.add)\
                           .then_inc(q("gru_cand"), 1)
                        after(eng, "gru_n", l, c + 1)
                        st.do(vec.tensor_tensor(tmp[:, 6, :], chunk(h, c), tmp[:, 3, :], ALU.subtract))
                        st.do(vec.tensor_tensor(tmp[:, 7, :], tmp[:, 6, :], tmp[:, 1, :], ALU.mult))
                        after(eng, "gru_h", l, c + 1)
                        vec.tensor_tensor(tmp[:, 5, :], tmp[:, 7, :], tmp[:, 3, :], ALU.add)\
                           .then_inc(q("gru_mixed"), 1)
                        st.do(vec.engine_nop())
                    st.leave(NCH // 2)

            def chunks_plus(name, b):
                eng.sem_inc(q(f"{name}_used"), 2)
                with eng.Fori(0, NCH // 2) as it:
                    for p in range(2):
                        c = it * 2 + p
                        eng.wait_ge(q(f"{name}_mm"), c + 1)
                        vec.scalar_tensor_tensor(out=chunk(acc, c), in0=ps[:, 4 + p, 0:CH], scalar=bs(b),
                                                 in1=chunk(x, c), op0=ALU.add, op1=ALU.add).then_inc(q(f"{name}_used"), 1)
                eng.wait_ge(q(f"{name}_used"), 2 + NCH)

            def norm(n):
                eng.sem_inc(q("ln_free"), 2)
                vec.engine_nop().then_inc(q("ln_in"), 1)
                with eng.Fori(0, NCH // 2) as it:
                    st.enter(it, 2)
                    for p in range(2):
                        c = it * 2 + p
                        after(eng, "ln_sd", n, c + 1)
                        st.do(vec.reciprocal(tmp[:, 4 + p, :], tmp[:, 2 + p, :]))
                        vec.tensor_tensor(chunk(x, c), ps[:, p, 0:CH], tmp[:, 4 + p, :], ALU.mult)\
                           .then_inc(q("ln_out"), 1)
                        after(eng, "ln_out", n, c + 1)
                        eng.sem_inc(q("ln_free"), 1)
                    st.leave(NCH // 2)

            def rank():
                with eng.Fori(0, HPAIRS) as it:
                    st.enter(it, 6)
                    for p in range(2):
                        cols = ds((it * 2 + p) * HT, HT)
                        hi1h = big[:, p, 0:HW].rearrange("p (k c) -> p k c", c=NB)
                        vec.tensor_tensor(hi1h, over_lanes(iota[:, 0:NB], HT), over_tiles(src_hi[:, cols], NB),
                                          ALU.is_equal).then_inc(q("rank_h"), 1)
                        eng.wait_ge(q("rank_mm"), it * 2 + p + 1)
                        prod = big[:, p, 2 * HW:3 * HW].rearrange("p (k c) -> p k c", c=NB)
                        st.do(vec.tensor_tensor(prod, hi1h, ps[:, p, 0:HW].rearrange("p (k c) -> p k c", c=NB), ALU.mult))
                        st.do(vec.tensor_reduce(slot[:, cols], prod, AX.X, ALU.add))
                        st.do(vec.tensor_copy(totals[:, cols], ps[0:NB, 2 + p, 0:HT]))
                    st.leave(HPAIRS)
                st.do(vec.tensor_tensor_scan(scanned, totals, totals, 0.0, ALU.add, ALU.bypass))
                st.do(vec.tensor_copy(blk_i[:, 0:1], scanned[:, NT - 1:NT]))
                st.do(vec.tensor_scalar(blk[:, 2:3], scanned[:, NT - 1:NT], float(P - 1), None, ALU.add))
                st.do(vec.tensor_copy(blk_i[:, 0:1], blk[:, 2:3]))
                st.do(vec.tensor_scalar(blk_i[:, 1:2], blk_i[:, 0:1], -P, None, ALU.bitwise_and))
                vec.tensor_copy(blk[:, 1:2], blk_i[:, 1:2]).then_inc(q("block_size"), 1)
                eng.wait_ge(q("block_start"), 1)
                st.did(vec.tensor_tensor(blk[:, 3:4], ps[0:NB, 4, 0:1], blk[:, 1:2], ALU.add))
                st.did(vec.tensor_tensor(totals, scanned, totals, ALU.subtract))
                st.settle()
                st.do(vec.tensor_scalar(totals, totals, ps[0:NB, 4, 0:1], None, ALU.add))
                st.did(vec.tensor_scalar(flat[0:NB, 512:512 + ST], iota[0:NB, 0:ST], float(P), None, ALU.mult))
                st.settle()
                vec.tensor_scalar(flat[0:NB, 0:ST], flat[0:NB, 512:512 + ST], blk[:, 3:4], None, ALU.is_ge)\
                   .then_inc(q("block_ended"), 1)
                eng.wait_ge(q("tile_block"), 1)
                st.do(vec.tensor_scalar(gcn_base[:], ps[:, 5, 0:ST], float(P), float(NP - P), ALU.mult, ALU.min))
                with eng.Fori(0, HPAIRS) as it:
                    st.enter(it, 8)
                    for p in range(2):
                        cols = ds((it * 2 + p) * HT, HT)
                        hi1h = big[:, p, 0:HW].rearrange("p (k c) -> p k c", c=NB)
                        vec.tensor_tensor(big[0:NB, p, HW:2 * HW].rearrange("p (k c) -> p k c", c=NB),
                                          over_lanes(w[0:NB, W_AT["ident"]:W_AT["ident"] + NB], HT, NB),
                                          over_tiles(totals[:, cols], NB), ALU.mult).then_inc(q("rank_diag"), 1)
                        st.do(vec.tensor_tensor(hi1h, over_lanes(iota[:, 0:NB], HT), over_tiles(src_hi[:, cols], NB),
                                                ALU.is_equal))
                        eng.wait_ge(q("rank_base"), it * 2 + p + 1)
                        prod = big[:, p, 2 * HW:3 * HW].rearrange("p (k c) -> p k c", c=NB)
                        st.do(vec.tensor_tensor(prod, hi1h, ps[:, p, 0:HW].rearrange("p (k c) -> p k c", c=NB), ALU.mult))
                        st.do(vec.tensor_reduce(slot_tile[:, cols], prod, AX.X, ALU.add))
                        st.do(vec.tensor_tensor(slot[:, cols], slot[:, cols], slot_tile[:, cols], ALU.add))
                    st.leave(HPAIRS)
                st.do(vec.tensor_copy(slot_i[:], slot[:]))
                st.do(vec.tensor_scalar(src[:], slot_i[:], P - 1, None, ALU.bitwise_and))
                st.do(vec.tensor_copy(slot_lane[:], src[:]))
                st.do(vec.tensor_scalar(src[:], slot_i[:], 7, None, ALU.arith_shift_right))
                st.do(vec.tensor_copy(slot_tile[:], src[:]))

            prep()
            for l in range(2):
                table(l)
                edge_sums(l)
                gru(l)
            after(eng, "gru_h", 1, 1 + NCH)
            chunks_plus("out", "out")
            norm(0)
            for k in range(2, 5):
                table(k)
                if k == 3:
                    for p in range(2):
                        after(eng, f"table_stored_{p}", k, 16 * (NB // 2))
                    rank()
                edge_sums(k)
                vec.scalar_tensor_tensor(out=h[:], in0=acc[:], scalar=0.0, in1=res[:], op0=ALU.max, op1=ALU.add)\
                   .then_inc(q("hidden"), 1)
                if k == 2:
                    after(eng, "extra_used", 2, 2 + NG)
                    st.do(vec.tensor_copy(by_src[:], ps[:, 7, 0:MV]))
                    st.do(vec.tensor_scalar(deg[:, 0, :], by_src[:, NB * A:MV], 1.0, None, ALU.max))
                    vec.tensor_scalar(deg[:, 2, :], by_src[:, NB * A:MV], 0.0, None, ALU.is_gt).then_inc(q("deg1"), 1)
                    eng.wait_ge(q("deg1"), 1)
                    st.did(vec.reciprocal(deg[:, 3, :], deg[:, 0, :]))
                    eng.wait_ge(q("deg_sqrt"), 1)
                    st.do(vec.reciprocal(dinv[:], deg[:, 1, :]))
                    st.do(vec.tensor_tensor(dinv[:], dinv[:], deg[:, 2, :], ALU.mult))
                    sums = by_src[:, 0:NB * A].rearrange("p (b a) -> p b a", a=A)
                    st.do(vec.tensor_tensor(sums, sums, over_tiles(deg[:, 3, :], A), ALU.mult))
                if k == 3:
                    after(eng, "extra_used", 3, 2 + NG)
                    st.do(vec.tensor_copy(scratch_i, ps[:, 7, 0:ST]))
                    st.do(vec.tensor_scalar(gcn_idx[:], scratch_i, 4095, None, ALU.bitwise_and))
                    st.do(vec.tensor_scalar(scratch_i, scratch_i, 12, None, ALU.arith_shift_right))
                    st.do(vec.tensor_scalar(gcn_lo[:], scratch_i, -1.0, None, ALU.add))
            after(eng, "hidden", 4, 1)
            st.do(vec.tensor_tensor(acc[:], h[:], x[:], ALU.add))
            norm(1)
            edge_sums(FLUSH)
            eng.wait_ge(q("dinv_mm"), 1)
            st.do(vec.tensor_tensor(acc[:], acc[:], psf[:, 0:NP], ALU.mult))
            st.do(vec.scalar_tensor_tensor(out=acc[:], in0=acc[:], scalar=bs("gcn"), in1=x[:], op0=ALU.add, op1=ALU.add))
            norm(2)
            eng.wait_ge(q("dst_count_mm"), 1)
            counts = ps[:, :, 0:CH]
            inv = flat[:, 0:NP].rearrange("p (c n) -> p c n", n=CH)
            st.do(vec.tensor_scalar(inv, counts, 1.0, None, ALU.max))
            st.do(vec.reciprocal(flat[:, 0:NP], flat[:, 0:NP]))
            vec.tensor_tensor(nodes[:], nodes[:], flat[:, 0:NP], ALU.mult).then_inc(q("nodes_ready"), 1)
            with eng.Fori(0, NCH // 2) as it:
                for p in range(2):
                    c = it * 2 + p
                    eng.wait_ge(q("mlp_pre"), c + 1)
                    vec.scalar_tensor_tensor(out=tmp[:, 2 + p, :], in0=tmp[:, p, :], scalar=0.01, in1=tmp[:, p, :],
                                             op0=ALU.mult, op1=ALU.max).then_inc(q("mlp_hidden"), 1)
                    eng.wait_ge(q("mlp2_mm"), c + 1)
                    vec.scalar_tensor_tensor(out=chunk(acc, c), in0=ps[:, 2 + p, 0:CH], scalar=bs("mlp2"),
                                             in1=chunk(x, c), op0=ALU.add, op1=ALU.add).then_inc(q("mlp_used"), 1)
            eng.wait_ge(q("mlp_used"), 2 + NCH)
            norm(3)


def _layout(v):
    f32 = np.float32

    def tiles(a, fill):
        full = np.full((NT * P,) + a.shape[1:], fill, a.dtype)
        full[:EDGES] = a
        return full

    def lanes(a):
        return np.ascontiguousarray(tiles(a, NONE).reshape(NT, P).T)

    blocks = {"proj": v["L0_gnn_node_proj_w"].T, "out": v["L0_gnn_out_w"].T, "res": v["L1_gnn_res_w"],
              "gcn": v["L2_gnn_W"].T, "w1x": v["L3_gnn_W1"][:P], "w2": v["L3_gnn_W2"]}
    cols = {"proj": v["L0_gnn_node_proj_b"], "out": v["L0_gnn_out_b"], "res": v["L1_gnn_res_b"],
            "gcn": v["L2_gnn_b"], "mlp1": v["L3_gnn_b1"], "mlp2": v["L3_gnn_b2"], "eps": np.full(P, EPS, f32)}
    for l in range(2):
        for t in range(T):
            blocks[f"edge{l}_{t}"] = v["L0_gnn_edge_W"][l, t].T
        for i, g in enumerate("rzn"):
            part = slice(i * P, (i + 1) * P)
            blocks[f"wih{l}_{g}"] = v["L0_gnn_gru_wih"][l, part].T
            blocks[f"whh{l}_{g}"] = v["L0_gnn_gru_whh"][l, part].T
            cols[f"bih{l}_{g}"] = v["L0_gnn_gru_bih"][l, part]
            cols[f"bhh{l}_{g}"] = v["L0_gnn_gru_bhh"][l, part]
    for l in range(3):
        for t in range(T):
            blocks[f"rel{l}_{t}"] = v[f"L1_gnn_W{l + 1}"][t]
        blocks[f"root{l}"] = v[f"L1_gnn_root{l + 1}"]
        cols[f"b{l}"] = v[f"L1_gnn_b{l + 1}"]
    w1a = np.zeros((P, P), f32)
    w1a[SRC_ROWS] = v["L3_gnn_W1"][P:P + A]
    w1a[DST_ROWS.start + T:DST_ROWS.stop] = v["L3_gnn_W1"][P + A:]
    blocks["w1a"] = w1a
    blocks["ident"] = np.eye(P, dtype=f32)
    blocks["mean"] = np.full((P, P), 1 / P, f32)
    blocks["center"] = np.eye(P, dtype=f32) - np.full((P, P), 1 / P, f32)
    blocks["before"] = np.triu(np.ones((P, P), f32), 1)
    blocks["ones"] = np.ones((P, P), f32)
    count = np.zeros((P, P), f32)
    count[DST_ROWS.start:DST_ROWS.start + T, DST_ROWS] = 1
    blocks["dst_count"] = count

    xT = np.zeros((P, NP), f32)
    xT[:, :NODES] = v["x"].T
    marks = np.zeros((NT * P, TC), f32)
    marks[:EDGES, T:] = v["edge_attr_16"]
    zero = np.zeros(P, f32)
    return {
        "xT": xT, "dst_rows": tiles(v["dst"], NONE).reshape(NG, GE), "dst_lanes": lanes(v["dst"]),
        "src_lanes": lanes(v["src"]), "typ_lanes": lanes(v["edge_type_8"]),
        "marks": np.ascontiguousarray(marks.reshape(NT, P, TC).transpose(1, 0, 2)).reshape(P, NT * TC),
        "weights": np.ascontiguousarray(np.concatenate([blocks[n] for n in W_NAMES], axis=1)),
        "biases": np.ascontiguousarray(np.stack([cols.get(n, zero) for n in B_NAMES], axis=1)),
        "iota": np.ascontiguousarray(np.broadcast_to(np.arange(512, dtype=f32), (P, 512))),
    }


def kernel(**inputs):
    import concourse.bacc as _bacc
    from concourse.bass_utils import run_bass_kernel_spmd as _run

    nc = _bacc.Bacc("TRN2", target_bir_lowering=False, num_devices=1)
    arrays = _layout({k: np.asarray(a) for k, a in inputs.items()})
    args = [nc.dram_tensor(f"in_{n}", a.shape, mybir.dt.from_np(a.dtype), kind="ExternalInput").ap()
            for n, a in arrays.items()]
    args.append(nc.dram_tensor("out_0", (P, NP), F32, kind="ExternalOutput").ap())
    graph_kernel(nc, *args)
    r = _run(nc, [{f"in_{n}": a for n, a in arrays.items()}], core_ids=[0])
    return np.ascontiguousarray(r.results[0]["out_0"][:, :NODES].T)
```

```python
from contextlib import ExitStack

import numpy as np
import concourse.bass as bass
from concourse import mybir

F32 = mybir.dt.float32
I32 = mybir.dt.int32
ALU = mybir.AluOpType
ACT = mybir.ActivationFunctionType
AX = mybir.AxisListType
ds = bass.ds

P = 128
NODES = 3125
EDGES = 53125
NB = 26
NP = NB * P
TB = 25
NV = TB * P
CB = 4
CH = CB * P
NCH = -(-TB // CB)
SLOTS = 4
T = 8
A = 16
TC = T + A
G = 8
GE = G * P
NG = -(-EDGES // GE)
NT = NG * G
SUB = 4
PASSES = NG // SUB
NONE = 8191
HW = G * NB
MV = NB * A + NB
ST = 448
SPASSES = ST // (SUB * G)
EPS = 1e-5
assert NG % SUB == 0 and NODES <= NV and NODES + P <= NP and MV <= 512
assert ST % (SUB * G) == 0 and ST * P >= EDGES + NB * (P - 1)

W_NAMES = (["proj"] + [f"edge{l}_{t}" for l in range(2) for t in range(T)]
           + [f"{s}{l}_{g}" for l in range(2) for s in ("wih", "whh") for g in "rzn"] + ["out", "res"]
           + [f"rel{l}_{t}" for l in range(3) for t in range(T)] + [f"root{l}" for l in range(3)]
           + ["gcn", "w1x", "w1a", "w2", "ident", "center", "mean", "before", "ones", "dst_count"])
W_AT = {n: i * P for i, n in enumerate(W_NAMES)}
B_NAMES = (["proj"] + [f"{s}{l}_{g}" for l in range(2) for s in ("bih", "bhh") for g in "rzn"]
           + [f"both{l}_{g}" for l in range(2) for g in "rz"]
           + ["out", "res", "b0", "b1", "b2", "gcn", "mlp1", "mlp2", "eps"])
B_AT = {n: i for i, n in enumerate(B_NAMES)}
INV_ROWS, DST_ROWS, SRC_ROWS = slice(0, T), slice(32, 32 + TC), slice(64, 64 + A)


class Steps:

    def __init__(self, eng, sem):
        self.eng, self.sem, self.base, self.j = eng, sem, 0, 0

    def did(self, ins):
        ins.then_inc(self.sem, 1)
        self.j += 1

    def settle(self):
        self.eng.wait_ge(self.sem, self.base + self.j)

    def do(self, ins):
        self.did(ins)
        self.settle()

    def enter(self, it, step):
        self.start, self.step, self.base, self.j = self.base + self.j, step, self.base + self.j + it * step, 0

    def leave(self, passes):
        assert self.j == self.step, self.j
        self.base, self.j = self.start + passes * self.step, 0


TOTALS = {
    "tab_mm": TB, "tab_act": TB, "tab_dve": TB, "h_ready": NCH, "root_mm": NCH, "root_used": NCH,
    "summed": SUB + NG, "onehot": 1 + NG, "added": 1 + NG, "gathered": 16 * G * PASSES, "idx_staged": NG,
    "marked": NG, "mark_loaded": 16 * PASSES, "zeros": 1, "opened": 1, "extra_ready": SUB + NG, "extra_used": 2 + NG,
    "gru_mm": NCH, "gru_rz": NCH, "gru_cand": NCH, "gru_n": NCH, "gru_mixed": NCH, "gru_h": NCH,
    "ln_in": NCH, "ln_center": NCH, "ln_sq": NCH, "ln_mean": NCH, "ln_sd": NCH, "ln_out": NCH,
}
FIRST_RUN = {"zeros": 2, "opened": 2, "extra_ready": 2, "extra_used": 2, "root_mm": 2, "root_used": 2}


def graph_kernel(nc, xT_d, dst_rows_d, dst_d, src_d, typ_d, mark_d, w_d, b_d, iota_d, out_d):
    with ExitStack() as ctx:
        def sb(name, shape, dt=F32):
            return ctx.enter_context(nc.sbuf_tensor(name, shape, dt))

        sems = {}

        def q(name):
            if name not in sems:
                sems[name] = ctx.enter_context(nc.semaphore(name))
            return sems[name]

        def after(eng, name, run, count):
            kind = name.rsplit("_", 1)[0] if name[-1].isdigit() else name
            eng.wait_ge(q(name), TOTALS[kind] * (run - FIRST_RUN.get(kind, 0)) + count)

        def stored(eng, k, b):
            s = b % SLOTS
            eng.wait_ge(q(f"table_stored_{s}"), 16 * (k * len(range(s, TB, SLOTS)) + b // SLOTS + 1))

        def all_stored(eng, k):
            for b in range(TB - SLOTS, TB):
                stored(eng, k, b)

        table_d = nc.dram_tensor("messages", (NV, T * P), F32).ap()
        gcn_table_d = nc.dram_tensor("gcn_rows", (NV, P), F32).ap()
        table_rows = table_d.rearrange("n (t d) -> (n t) d", t=T)

        ps = ctx.enter_context(nc.psum_tensor("ps", [P, 8, 512], F32))
        psf = ps[:].rearrange("p a b -> p (a b)")

        w = sb("w", [P, len(W_NAMES) * P])
        bias = sb("bias", [P, len(B_NAMES)])
        iota = sb("iota", [P, 512])
        x = sb("x", [P, NV])
        h = sb("h", [P, NV])
        res = sb("res", [P, NV])
        acc = sb("acc", [P, NP])
        nodes = sb("nodes", [P, NP])
        dst = sb("dst", [P, NT], I32)
        src = sb("src", [P, NT], I32)
        typ = sb("typ", [P, NT], I32)
        row_idx = sb("row_idx", [P, NT], I32)
        dst_lo = sb("dst_lo", [P, NT + G])
        src_lo = sb("src_lo", [P, NT])
        src_hi = sb("src_hi", [P, NT])
        typ_f = sb("typ_f", [P, NT])
        edge_w = sb("edge_w", [P, NT + G])
        base_f = sb("base_f", [P, NG])
        base_i = sb("base_i", [P, NG], I32)
        base_diag = sb("base_diag", [NG, NG])
        first = sb("first", [NG, 1])
        msg = sb("msg", [P, SUB, G, P])
        mark = sb("mark", [P, SUB, G * TC])
        idx_buf = sb("idx_buf", [P, SUB, G], I32)
        onehot = sb("onehot", [P, 2, G, P])
        lane1h = sb("lane1h", [P, 2, G, P])
        big = sb("big", [P, 2, G * ST])
        gcn_idx = sb("gcn_idx", [P, ST], I32)
        gcn_lo = sb("gcn_lo", [P, ST + G])
        gcn_base = sb("gcn_base", [P, ST], I32)
        slot = sb("slot", [P, NT])
        payload = sb("payload", [P, NT])
        by_src = sb("by_src", [P, MV])
        deg = sb("deg", [P, 4, NB])
        dinv = sb("dinv", [P, NB])
        blk = sb("blk", [NB, 4])
        blk_i = sb("blk_i", [NB, 2], I32)
        tmp = sb("tmp", [P, 8, CH])
        flat = big[:].rearrange("p a b -> p (a b)")
        slot_i, slot_tile, slot_lane, valid = typ, typ_f, src_hi, edge_w[:, 0:NT]
        spare = lane1h[0:NB, 1, :, :].rearrange("p a b -> p (a b)")
        totals, scanned = spare[:, 0:NT], spare[:, 512:512 + NT]
        TT, PROD, HI1H, HPROD, HDIAG = 0, GE, 4096, 4608, 5120
        rank1h = flat[:, HI1H:HI1H + HW]
        rank_prod = flat[:, HPROD:HPROD + HW]
        rank_diag = flat[0:NB, HDIAG:HDIAG + HW]

        def wt(name, n=1):
            return w[:, W_AT[name]:W_AT[name] + n * P]

        def bs(name):
            return bias[:, B_AT[name]:B_AT[name] + 1]

        def width(c):
            return min(CH, NV - c * CH)

        def chunk(buf, c):
            return buf[:, c * CH:c * CH + width(c)]

        def bank(i, c):
            return ps[:, i, 0:width(c)]

        def blocks_of(c):
            return range(c * CB, min(c * CB + CB, TB))

        def block_of(buf, b):
            return buf[:, b * P:(b + 1) * P]

        def by_group(buf, cols):
            return buf.rearrange("p (k c) -> p k c", c=cols)

        loops = [
            (row_idx, dst_lo, False, table_rows, PASSES, "count"),
            (row_idx, dst_lo, False, table_rows, PASSES, "weigh"),
            (row_idx, dst_lo, True, table_rows, PASSES, "attr_by_src"),
            (row_idx, dst_lo, True, table_rows, PASSES, "scatter"),
            (row_idx, dst_lo, True, table_rows, PASSES, None),
            (gcn_idx, gcn_lo, False, gcn_table_d, SPASSES, None),
        ]
        mark_free = {0: "count_mm", 1: "turned", 2: "extra_ready"}
        BY_SRC = 5

        block = ctx.enter_context(nc.Block())

        @block.sync
        def _(eng):
            eng.dma_start(bias[:], b_d).then_inc(q("loaded_x"), 16)
            eng.dma_start(w[:, 0:P], w_d[:, 0:P]).then_inc(q("loaded_x"), 16)
            eng.dma_start(x[:], xT_d).then_inc(q("loaded_x"), 16)
            eng.dma_start(w[:, P:], w_d[:, P:]).then_inc(q("loaded_w"), 16)
            eng.dma_start(flat[0:NG, 6144:6144 + GE].bitcast(I32), dst_rows_d).then_inc(q("loaded"), 16)
            for buf, d in ((dst, dst_d), (src, src_d), (typ, typ_d), (iota, iota_d)):
                eng.dma_start(buf[:], d).then_inc(q("loaded"), 16)

            for k in range(5):
                for b in range(TB):
                    s = b % SLOTS
                    after(eng, "tab_act", k, b + 1)
                    after(eng, "tab_dve", k, b + 1)
                    eng.dma_start(table_d[b * P:(b + 1) * P, :], flat[:, s * 1024:(s + 1) * 1024])\
                       .then_inc(q(f"table_stored_{s}"), 16)
                if k in mark_free:
                    with eng.Fori(0, PASSES) as it:
                        for s in range(SUB):
                            eng.wait_ge(q(mark_free[k]), it * SUB + s + 1)
                            eng.dma_start(mark[:, s, :], mark_d[:, ds((it * SUB + s) * (G * TC), G * TC)])\
                               .then_inc(q(f"mark_loaded_{s}"), 16)
            for c in range(NCH):
                n = len(blocks_of(c))
                eng.wait_ge(q("gcn_rows"), c + 1)
                eng.dma_start(gcn_table_d[c * CH:c * CH + width(c), :].rearrange("(b p) d -> p b d", p=P),
                              chunk(flat, c).rearrange("p (b d) -> p b d", d=P)).then_inc(q("gcn_stored"), 16)
            for c in range(NCH):
                eng.wait_ge(q("n3_out"), c + 1)
                eng.dma_start(chunk(out_d, c), chunk(x, c)).then_inc(q("out_stored"), 16)
            eng.wait_ge(q("out_stored"), 16 * NCH)

        @block.gpsimd
        def _(eng):
            st = Steps(eng, q("pool_steps"))
            for k, (idx, lo, weighted, table, passes, extra) in enumerate(loops):
                if k == 0:
                    eng.wait_ge(q("rows_ready"), 1)
                if k == BY_SRC:
                    eng.wait_ge(q("gcn_stored"), 16 * NCH)
                else:
                    all_stored(eng, k)
                with eng.Fori(0, passes) as it:
                    st.enter(it, SUB if extra == "weigh" else 0)
                    for s in range(SUB):
                        if extra == "weigh":
                            after(eng, "summed", k, it * SUB + s + 1)
                            st.do(eng.tensor_copy(idx_buf[:, s, :], idx[:, ds((it * SUB + s) * G, G)]))
                        else:
                            after(eng, "idx_staged", k - (k > 1), it * SUB + s + 1)
                        eng.sem_inc(q("rows_known"), 1)
                        for t in range(G):
                            eng.indirect_dma_start(msg[:, s, t, :], None, table,
                                                   bass.IndirectOffsetOnAxis(ap=idx_buf[:, s, t:t + 1], axis=0))\
                               .then_inc(q(f"gathered_{s}"), 16)
                    st.leave(passes)

        @block.tensor
        def _(eng):
            mm = eng.matmul

            def table(k, weight, source, c):
                for b in blocks_of(c):
                    p = b % 2
                    if b >= 2:
                        after(eng, "tab_act", k, b - 1)
                        after(eng, "tab_dve", k, b - 1)
                    mm(ps[:, 2 * p, :], block_of(source, b), wt(weight, T)[:, 0:512], start=True, stop=True)
                    mm(ps[:, 2 * p + 1, :], block_of(source, b), wt(weight, T)[:, 512:1024], start=True, stop=True)\
                        .then_inc(q("tab_mm"), 1)

            def edge_sums(k):
                idx, lo, weighted, tab, passes, extra = loops[k]
                wide = extra in ("attr_by_src", "scatter")
                n = MV if extra == "attr_by_src" else ST
                eng.sem_inc(q("summed"), SUB)
                if extra == "count":
                    eng.sem_inc(q("count_mm"), SUB)
                if extra == "weigh":
                    eng.sem_inc(q("turned"), SUB)
                    eng.sem_inc(q("weigh_mm"), 1)
                    eng.wait_ge(q("inv_ready"), 1)
                if wide:
                    after(eng, "zeros", k, 1)
                    mm(ps[:, 7, 0:n], wt("ones"), flat[:, G * ST:G * ST + n], start=True, stop=False,
                       skip_group_check=True).then_inc(q("opened"), 1)
                    eng.sem_inc(q("extra_used"), 2)
                with eng.Fori(0, passes) as it:
                    for s in range(SUB):
                        g = it * SUB + s
                        if extra == "weigh":
                            base = eng.value_load(base_i[0:1, ds(g, 1)], min_val=0, max_val=NP - P)
                        after(eng, "onehot", k, g + 1)
                        after(eng, f"gathered_{s}", k, (it + 1) * (16 * G))
                        for t in range(G):
                            if k == BY_SRC:
                                out = ps[:, 2 * (s % 2) + t // 4, (t % 4) * P:(t % 4) * P + P]
                                last = mm(out, msg[:, s, t, :], onehot[:, s % 2, t, :], start=True, stop=True)
                            else:
                                last = mm(ps[:, s % 2, 0:P], msg[:, s, t, :], onehot[:, s % 2, t, :],
                                          start=t == 0, stop=t == G - 1)
                        last.then_inc(q("summed"), 1)
                        if extra == "count":
                            eng.wait_ge(q("marked"), g + 1)
                            for t in range(G):
                                last = mm(ps[DST_ROWS, 2 + s % 2, 0:P], mark[:, s, t * TC:(t + 1) * TC],
                                          onehot[:, s % 2, t, :], start=t == 0, stop=t == G - 1)
                            last.then_inc(q("count_mm"), 1)
                            eng.wait_ge(q("rank_1h"), g + 1)
                            for t in range(G):
                                mm(ps[0:NB, 5, t:t + 1], rank1h[:, t * NB:(t + 1) * NB], wt("ones")[:, 0:1],
                                   start=True, stop=True)
                            mm(ps[:, 4, 0:HW], wt("before"), rank1h, start=True, stop=True).then_inc(q("rank_mm"), 1)
                        if extra == "weigh":
                            after(eng, "marked", 1, g + 1)
                            for t in range(G):
                                last = mm(ps[0:T, 2 + t // 4, (t % 4) * P:(t % 4) * P + P],
                                          mark[:, s, t * TC:t * TC + T], wt("ident"), start=True, stop=True)
                            last.then_inc(q("turned"), 1)
                            eng.wait_ge(q("rank_diag"), g + 1)
                            mm(ps[:, 6, 0:HW], w[0:NB, W_AT["ones"]:W_AT["ones"] + P], rank_diag, start=True,
                               stop=True).then_inc(q("rank_base"), 1)
                            eng.wait_ge(q("turned_copied"), g + 1)
                            eng.wait_ge(q("weighed"), g + 1)
                            for t in range(G):
                                last = mm(ps[:, 4 + t // 4, (t % 4) * P:(t % 4) * P + P],
                                          flat[INV_ROWS, TT + t * P:TT + (t + 1) * P], nodes[INV_ROWS, ds(base, P)],
                                          start=True, stop=True)
                            last.then_inc(q("weigh_mm"), 1)
                        if wide:
                            after(eng, "extra_ready", k, g + 1 + SUB * (k == 2))
                            for t in range(G):
                                last = mm(ps[:, 7, 0:n], lane1h[:, s % 2, t, :], big[:, s % 2, t * ST:t * ST + n],
                                          start=False, stop=False, skip_group_check=True)
                            last.then_inc(q("extra_used"), 1)

            def gru(l, c):
                if c >= 1:
                    after(eng, "gru_rz", l, c)
                    after(eng, "gru_cand", l, c)
                for i, (a, b) in enumerate((("wih", "r"), ("wih", "z"), ("wih", "n"), ("whh", "n"))):
                    last = mm(bank(4 + i, c), wt(f"{a}{l}_{b}"), chunk(acc if a == "wih" else h, c),
                              start=True, stop=i >= 2)
                    if i < 2:
                        last = mm(bank(4 + i, c), wt(f"whh{l}_{b}"), chunk(h, c), start=False, stop=True)
                last.then_inc(q("gru_mm"), 1)

            eng.wait_ge(q("loaded_x"), 3 * 16)
            for i in range(NCH + 1):
                if i < NCH:
                    if i >= 2:
                        after(eng, "h_ready", 0, i - 1)
                    mm(bank(4 + i % 2, i), wt("proj"), chunk(x, i), start=True, stop=True).then_inc(q("proj_mm"), 1)
                if i == 1:
                    eng.wait_ge(q("loaded_w"), 16)
                if i >= 1:
                    after(eng, "h_ready", 0, i)
                    table(0, "edge0_0", h, i - 1)
            eng.wait_ge(q("diag_ready"), 1)
            mm(ps[:, 7, 0:NG], w[0:NG, W_AT["ones"]:W_AT["ones"] + P], base_diag[:], start=True, stop=True)\
                .then_inc(q("base_mm"), 1)
            eng.wait_ge(q("rows_ready"), 1)
            edge_sums(0)
            after(eng, "added", 0, 1 + NG)
            eng.wait_ge(q("loop_done"), 1)
            for i in range(NCH + 1):
                if i < NCH:
                    gru(0, i)
                if i >= 1:
                    after(eng, "gru_h", 0, i)
                    table(1, "edge1_0", h, i - 1)
            eng.wait_ge(q("block_size"), 1)
            mm(ps[0:NB, 6, 0:1], w[0:NB, W_AT["before"]:W_AT["before"] + NB], blk[:, 1:2], start=True, stop=True)\
                .then_inc(q("block_start"), 1)
            eng.wait_ge(q("block_ended"), 1)
            mm(ps[:, 7, 0:ST], w[0:NB, W_AT["ones"]:W_AT["ones"] + P], flat[0:NB, HI1H:HI1H + ST], start=True, stop=True)\
                .then_inc(q("tile_block"), 1)
            edge_sums(1)
            after(eng, "added", 1, 1 + NG)
            eng.wait_ge(q("loop_done"), 2)
            for i in range(NCH + 3):
                if i < NCH:
                    gru(1, i)
                if 1 <= i < NCH + 1:
                    c = i - 1
                    after(eng, "gru_h", 1, c + 1)
                    if c >= 1:
                        after(eng, "ln_in", 0, c)
                    mm(bank(3, c), wt("out"), chunk(h, c), start=True, stop=True)\
                        .then_inc(q("out_mm"), 1)
                if 2 <= i < NCH + 2:
                    c = i - 2
                    after(eng, "ln_in", 0, c + 1)
                    if c >= 1:
                        eng.wait_ge(q("ln_kept"), c)
                        after(eng, "ln_sq", 0, c)
                    mm(bank(0, c), wt("center"), chunk(acc, c), start=True, stop=True).then_inc(q("ln_center"), 1)
                if 3 <= i:
                    c = i - 3
                    after(eng, "ln_sq", 0, c + 1)
                    if c >= 1:
                        eng.wait_ge(q("var_kept"), c)
                    mm(bank(2, c), wt("mean"), tmp[:, c % 2, 0:width(c)], start=True, stop=True)\
                        .then_inc(q("ln_mean"), 1)
            eng.wait_ge(q("var_kept"), NCH)
            for c in range(NCH):
                after(eng, "ln_out", 0, c + 1)
                if c >= 2:
                    eng.wait_ge(q("res_used"), c - 1)
                mm(bank(4 + c % 2, c), wt("res"), chunk(x, c), start=True, stop=True).then_inc(q("res_mm"), 1)
                table(2, "rel0_0", x, c)
            eng.wait_ge(q("res_used"), NCH)
            for k in range(2, 5):
                source = x if k == 2 else h
                if k > 2:
                    for c in range(NCH):
                        after(eng, "h_ready", k - 2, c + 1)
                        table(k, f"rel{k - 2}_0", h, c)
                for c in range(NCH):
                    if c >= 2:
                        after(eng, "root_used", k, c - 1)
                    mm(bank(4 + c % 2, c), wt(f"root{k - 2}"), chunk(source, c), start=True, stop=True)\
                        .then_inc(q("root_mm"), 1)
                after(eng, "root_used", k, NCH)
                edge_sums(k)
            for i in range(NCH + 2):
                if i < NCH:
                    after(eng, "ln_in", 1, i + 1)
                    if i >= 2:
                        after(eng, "ln_out", 1, i - 1)
                    mm(bank(i % 2, i), wt("center"), chunk(acc, i), start=True, stop=True).then_inc(q("ln_center"), 1)
                if 1 <= i < NCH + 1:
                    c = i - 1
                    after(eng, "ln_sq", 1, c + 1)
                    if c >= 2:
                        after(eng, "ln_sd", 1, c - 1)
                    mm(bank(2 + c % 2, c), wt("mean"), tmp[:, c % 2, 0:width(c)], start=True, stop=True)\
                        .then_inc(q("ln_mean"), 1)
                if i >= 2:
                    c = i - 2
                    after(eng, "ln_out", 1, c + 1)
                    if c >= 2:
                        eng.wait_ge(q("gcn_rows"), c - 1)
                    for b in blocks_of(c):
                        last = mm(ps[:, 4 + c % 2, (b % CB) * P:(b % CB + 1) * P], block_of(x, b), wt("gcn"),
                                  start=True, stop=True)
                    last.then_inc(q("gcn_mm"), 1)
            eng.wait_ge(q("gcn_rows"), NCH)
            for c in range(NCH):
                if c >= 2:
                    eng.wait_ge(q("dinv_used"), c - 1)
                for b in blocks_of(c):
                    last = mm(ps[:, 4 + c % 2, (b % CB) * P:(b % CB + 1) * P],
                              dinv[:, b:b + 1].to_broadcast([P, P]), wt("ident"), start=True, stop=True)
                last.then_inc(q("dinv_mm"), 1)
            for c in range(NCH):
                if c >= 2:
                    eng.wait_ge(q("turn_used"), c - 1)
                for b in blocks_of(c):
                    last = mm(ps[SRC_ROWS, 6 + c % 2, (b % CB) * P:(b % CB + 1) * P], by_src[:, b * A:(b + 1) * A],
                              wt("ident"), start=True, stop=True)
                last.then_inc(q("turn_mm"), 1)
            eng.wait_ge(q("dinv_used"), NCH)
            eng.wait_ge(q("turn_used"), NCH)
            for c in range(NCH):
                if c >= 2:
                    eng.wait_ge(q("by_dst_mean"), c - 1)
                mm(bank(4 + c % 2, c), wt("dst_count"), chunk(nodes, c), start=True, stop=True)\
                    .then_inc(q("dst_count_mm"), 1)
            edge_sums(BY_SRC)
            after(eng, "added", BY_SRC, 1 + ST)
            eng.wait_ge(q("by_dst_mean"), NCH)
            for i in range(NCH + 6):
                if i < NCH:
                    eng.wait_ge(q("n2_in"), i + 1)
                    if i >= 2:
                        eng.wait_ge(q("n2_out"), i - 1)
                    mm(bank(6 * (i % 2), i), wt("center"), chunk(acc, i), start=True, stop=True).then_inc(q("n2_center"), 1)
                if 1 <= i < NCH + 1:
                    c = i - 1
                    eng.wait_ge(q("n2_sq"), c + 1)
                    if c >= 1:
                        eng.wait_ge(q("n2_sd"), c)
                    mm(bank(1, c), wt("mean"), tmp[:, 0, 0:width(c)], start=True, stop=True).then_inc(q("n2_mean"), 1)
                if 2 <= i < NCH + 2:
                    c = i - 2
                    eng.wait_ge(q("n2_out"), c + 1)
                    if c >= 1:
                        eng.wait_ge(q("mlp_pre"), c)
                    mm(bank(2, c), wt("w1x"), chunk(x, c), start=True, stop=False)
                    mm(bank(2, c), wt("w1a"), chunk(nodes, c), start=False, stop=True).then_inc(q("mlp1_mm"), 1)
                if 3 <= i < NCH + 3:
                    c = i - 3
                    eng.wait_ge(q("mlp_hidden"), c + 1)
                    if c >= 1:
                        eng.wait_ge(q("n3_in"), c)
                    mm(bank(3, c), wt("w2"), tmp[:, 3, 0:width(c)], start=True, stop=True).then_inc(q("mlp2_mm"), 1)
                if 4 <= i < NCH + 4:
                    c = i - 4
                    eng.wait_ge(q("n3_in"), c + 1)
                    if c >= 2:
                        eng.wait_ge(q("n3_out"), c - 1)
                    mm(bank(4 + 3 * (c % 2), c), wt("center"), chunk(acc, c), start=True, stop=True).then_inc(q("n3_center"), 1)
                if 5 <= i < NCH + 5:
                    c = i - 5
                    eng.wait_ge(q("n3_sq"), c + 1)
                    if c >= 1:
                        eng.wait_ge(q("n3_sd"), c)
                    mm(bank(5, c), wt("mean"), tmp[:, 4, 0:width(c)], start=True, stop=True).then_inc(q("n3_mean"), 1)

        @block.scalar
        def _(eng):
            act = nc.scalar.activation

            def table(k, c, some=slice(None)):
                for b in blocks_of(c)[some] if 0 <= c < NCH else ():
                    after(eng, "tab_mm", k, b + 1)
                    if b >= SLOTS:
                        stored(eng, k, b - SLOTS)
                    s = b % SLOTS
                    act(flat[:, s * 1024:s * 1024 + 512], ps[:, 2 * (b % 2), :], ACT.Copy).then_inc(q("tab_act"), 1)

            def stage_rows(k):
                idx, passes = loops[k][0], loops[k][4]
                with eng.Fori(0, passes) as it:
                    for s in range(SUB):
                        after(eng, "summed", k, it * SUB + s + 1)
                        act(idx_buf[:, s, :], idx[:, ds((it * SUB + s) * G, G)], ACT.Copy).then_inc(q("idx_staged"), 1)

            def gru(l, i, between=lambda some: None):
                if i < NCH:
                    after(eng, "gru_mm", l, i + 1)
                    if i >= 2:
                        after(eng, "gru_mixed", l, i - 1)
                    act(tmp[:, 2 + i % 2, 0:width(i)], bank(4, i), ACT.Sigmoid, bias=bs(f"both{l}_r"))
                    act(tmp[:, 4 + i % 2, 0:width(i)], bank(5, i), ACT.Sigmoid, bias=bs(f"both{l}_z"))\
                        .then_inc(q("gru_rz"), 1)
                    between(slice(0, 1))
                    after(eng, "gru_cand", l, i + 1)
                    act(tmp[:, 6, 0:width(i)], tmp[:, 6, 0:width(i)], ACT.Tanh, bias=bs(f"bih{l}_n"))\
                        .then_inc(q("gru_n"), 1)
                    between(slice(1, 2))
                    after(eng, "gru_mixed", l, i + 1)
                    act(chunk(h, i), tmp[:, 7, 0:width(i)], ACT.Relu).then_inc(q("gru_h"), 1)
                    between(slice(2, None))
                else:
                    between(slice(None))

            eng.wait_ge(q("loaded_x"), 3 * 16)
            for i in range(NCH + 1):
                if i < NCH:
                    eng.wait_ge(q("proj_mm"), i + 1)
                    act(chunk(h, i), bank(4 + i % 2, i), ACT.Relu, bias=bs("proj")).then_inc(q("h_ready"), 1)
                if i >= 1:
                    table(0, i - 1)
            eng.wait_ge(q("rows_ready"), 1)
            stage_rows(0)
            for i in range(NCH + 1):
                gru(0, i, lambda some: table(1, i - 1, some))
            all_stored(eng, 1)
            with eng.Fori(0, PASSES) as it:
                for s in range(SUB):
                    g = it * SUB + s
                    eng.wait_ge(q("turned"), g + 1 + SUB)
                    eng.wait_ge(q("weigh_mm"), g + 1)
                    act(flat[0:T, TT:TT + GE], psf[0:T, 1024:1024 + GE], ACT.Copy).then_inc(q("turned_copied"), 1)
            for i in range(NCH + 3):
                gru(1, i)
                if 2 <= i < NCH + 2:
                    c = i - 2
                    after(eng, "ln_center", 0, c + 1)
                    if c >= 2:
                        after(eng, "ln_mean", 0, c - 1)
                    act(tmp[:, c % 2, 0:width(c)], bank(0, c), ACT.Square).then_inc(q("ln_sq"), 1)
                if 3 <= i:
                    c = i - 3
                    after(eng, "ln_mean", 0, c + 1)
                    act(chunk(res, c), bank(2, c), ACT.Copy).then_inc(q("var_kept"), 1)
            for i in range(NCH + 1):
                if i < NCH:
                    if i >= 2:
                        after(eng, "ln_out", 0, i - 1)
                    eng.wait_ge(q("var_kept"), i + 1)
                    act(tmp[:, 2 + i % 2, 0:width(i)], chunk(res, i), ACT.Sqrt, bias=bs("eps")).then_inc(q("ln_sd"), 1)
                if i >= 1:
                    c = i - 1
                    eng.wait_ge(q("res_mm"), c + 1)
                    act(chunk(res, c), bank(4 + c % 2, c), ACT.Identity, bias=bs("res")).then_inc(q("res_used"), 1)
                    table(2, c)
            for k in range(2, 5):
                if k > 2:
                    for c in range(NCH):
                        table(k, c)
                for c in range(NCH):
                    after(eng, "root_mm", k, c + 1)
                    act(chunk(acc, c), bank(4 + c % 2, c), ACT.Identity, bias=bs(f"b{k - 2}")).then_inc(q("root_used"), 1)
                if k == 3:
                    eng.wait_ge(q("degree"), 1)
                    act(deg[:, 1, :], deg[:, 0, :], ACT.Sqrt).then_inc(q("deg_sqrt"), 1)
                stage_rows(k)
            for i in range(NCH + 1):
                if i < NCH:
                    after(eng, "ln_center", 1, i + 1)
                    if i >= 2:
                        after(eng, "ln_mean", 1, i - 1)
                    act(tmp[:, i % 2, 0:width(i)], bank(i % 2, i), ACT.Square).then_inc(q("ln_sq"), 1)
                if i >= 1:
                    c = i - 1
                    after(eng, "ln_mean", 1, c + 1)
                    if c >= 2:
                        after(eng, "ln_out", 1, c - 1)
                    act(tmp[:, 2 + c % 2, 0:width(c)], bank(2 + c % 2, c), ACT.Sqrt, bias=bs("eps"))\
                        .then_inc(q("ln_sd"), 1)
            for c in range(NCH):
                eng.wait_ge(q("dinv_mm"), c + 1)
                act(chunk(res, c), bank(4 + c % 2, c), ACT.Copy).then_inc(q("dinv_used"), 1)
            for c in range(NCH):
                eng.wait_ge(q("turn_mm"), c + 1)
                act(chunk(nodes, c)[SRC_ROWS], ps[SRC_ROWS, 6 + c % 2, 0:width(c)], ACT.Copy).then_inc(q("turn_used"), 1)
            stage_rows(BY_SRC)
            for i in range(NCH + 6):
                if i < NCH:
                    eng.wait_ge(q("n2_center"), i + 1)
                    if i >= 1:
                        eng.wait_ge(q("n2_mean"), i)
                    act(tmp[:, 0, 0:width(i)], bank(6 * (i % 2), i), ACT.Square).then_inc(q("n2_sq"), 1)
                if 1 <= i < NCH + 1:
                    c = i - 1
                    eng.wait_ge(q("n2_mean"), c + 1)
                    if c >= 1:
                        eng.wait_ge(q("n2_out"), c)
                    act(tmp[:, 1, 0:width(c)], bank(1, c), ACT.Sqrt, bias=bs("eps")).then_inc(q("n2_sd"), 1)
                if 2 <= i < NCH + 2:
                    c = i - 2
                    eng.wait_ge(q("mlp1_mm"), c + 1)
                    if c >= 1:
                        eng.wait_ge(q("mlp_hidden"), c)
                    act(tmp[:, 2, 0:width(c)], bank(2, c), ACT.Identity, bias=bs("mlp1")).then_inc(q("mlp_pre"), 1)
                if 4 <= i < NCH + 4:
                    c = i - 4
                    eng.wait_ge(q("n3_center"), c + 1)
                    if c >= 1:
                        eng.wait_ge(q("n3_mean"), c)
                    act(tmp[:, 4, 0:width(c)], bank(4 + 3 * (c % 2), c), ACT.Square).then_inc(q("n3_sq"), 1)
                if 5 <= i < NCH + 5:
                    c = i - 5
                    eng.wait_ge(q("n3_mean"), c + 1)
                    if c >= 1:
                        eng.wait_ge(q("n3_out"), c)
                    act(tmp[:, 5, 0:width(c)], bank(5, c), ACT.Sqrt, bias=bs("eps")).then_inc(q("n3_sd"), 1)

        @block.vector
        def _(eng):
            vec = nc.vector
            st = Steps(eng, q("dve_steps"))

            def over_tiles(buf, n):
                return buf.unsqueeze(2).to_broadcast([buf.shape[0], buf.shape[1], n])

            def over_lanes(row, n):
                return row.unsqueeze(1).to_broadcast([row.shape[0], n, row.shape[1]])

            def prep():
                eng.wait_ge(q("loaded"), 5 * 16)
                st.do(vec.tensor_reduce(first[:], flat[0:NG, 6144:6144 + GE].bitcast(I32), AX.X, ALU.min))
                eng.wait_ge(q("loaded_w"), 16)
                vec.tensor_scalar(base_diag[:], w[0:NG, W_AT["ident"]:W_AT["ident"] + NG], first[:], None, ALU.mult)\
                   .then_inc(q("diag_ready"), 1)
                st.did(vec.tensor_scalar(valid, src[:], float(NONE), None, ALU.is_lt))
                st.did(vec.tensor_copy(typ_f[:], typ[:]))
                st.settle()
                st.did(vec.tensor_scalar(slot_i[:], src[:], P - 1, None, ALU.bitwise_and))
                st.do(vec.scalar_tensor_tensor(out=slot[:], in0=src[:], scalar=float(T), in1=typ_f[:],
                                               op0=ALU.mult, op1=ALU.add))
                st.did(vec.tensor_copy(src_lo[:], slot_i[:]))
                st.did(vec.tensor_tensor(row_idx[:], slot[:], valid, ALU.mult))
                st.settle()
                st.do(vec.tensor_scalar(slot_i[:], src[:], 7, None, ALU.arith_shift_right))
                st.did(vec.tensor_copy(src_hi[:], slot_i[:]))
                st.do(vec.tensor_scalar(payload[:], src_lo[:], 1.0, 4096.0, ALU.add, ALU.mult))
                st.do(vec.tensor_tensor(payload[:], payload[:], dst[:], ALU.add))
                st.do(vec.tensor_tensor(payload[:], payload[:], valid, ALU.mult))
                for l in range(2):
                    for g in "rz":
                        st.did(vec.tensor_tensor(bs(f"both{l}_{g}"), bs(f"bih{l}_{g}"), bs(f"bhh{l}_{g}"), ALU.add))
                st.did(vec.memset(nodes[:], 0.0))
                st.did(vec.memset(dst_lo[:, NT:], -1.0))
                st.did(vec.memset(gcn_lo[:, ST:], -1.0))
                st.settle()
                st.did(vec.memset(edge_w[:, NT:], 0.0))

            def windows():
                eng.wait_ge(q("base_mm"), 1)
                st.did(vec.tensor_copy(base_f[:], ps[:, 7, 0:NG]))
                st.did(vec.tensor_copy(base_i[:], ps[:, 7, 0:NG]))
                st.settle()
                st.do(vec.tensor_tensor(by_group(dst_lo[:, 0:NT], G), by_group(dst[:], G), over_tiles(base_f[:], G),
                                        ALU.subtract))
                vec.engine_nop().then_inc(q("rows_ready"), 1)

            def table(k, c, some=slice(None)):
                for b in blocks_of(c)[some] if 0 <= c < NCH else ():
                    after(eng, "tab_mm", k, b + 1)
                    if b >= SLOTS:
                        stored(eng, k, b - SLOTS)
                    s = b % SLOTS
                    vec.tensor_copy(flat[:, s * 1024 + 512:(s + 1) * 1024], ps[:, 2 * (b % 2) + 1, :])\
                       .then_inc(q("tab_dve"), 1)

            def edge_sums(k):
                idx, lo, weighted, tab, passes, extra = loops[k]
                last_group = passes * SUB

                def spread(g, s):
                    if weighted:
                        for t in range(G):
                            last = vec.tensor_scalar(onehot[:, s % 2, t, :], iota[:, 0:P], lo[:, ds(g * G + t, 1)],
                                                     edge_w[:, ds(g * G + t, 1)], ALU.is_equal, ALU.mult)
                    else:
                        last = vec.tensor_tensor(onehot[:, s % 2, :, :], over_lanes(iota[:, 0:P], G),
                                                 over_tiles(lo[:, ds(g * G, G)], P), ALU.is_equal)
                    last.then_inc(q("onehot"), 1)

                if k in (0, 1, BY_SRC):
                    st.do(vec.memset(acc[:], 0.0))
                else:
                    st.do(vec.memset(acc[:, NV:], 0.0))
                    after(eng, "root_used", k, NCH)
                if k < BY_SRC:
                    all_stored(eng, k)
                if extra in ("attr_by_src", "scatter"):
                    vec.memset(flat[:, G * ST:G * ST + 512], 0.0).then_inc(q("zeros"), 1)
                    after(eng, "opened", k, 1)
                if k == 2:
                    eng.sem_inc(q("extra_ready"), SUB)
                eng.sem_inc(q("added"), 1)
                if extra == "count":
                    eng.sem_inc(q("counted"), 1)
                if extra == "weigh":
                    eng.sem_inc(q("weighed"), 1)
                spread(0, 0)
                with eng.Fori(0, passes) as it:
                    st.enter(it, {"count": 3 * SUB, "weigh": 4 * SUB, "attr_by_src": 2 * SUB}.get(extra, 0))
                    for s in range(SUB):
                        g = it * SUB + s
                        if k != BY_SRC:
                            bases = [eng.value_load(base_i[0:1, ds(g, 1)], min_val=0, max_val=NP - P)]
                        else:
                            bases = [eng.value_load(gcn_base[0:1, ds(g * G + t, 1)], min_val=0, max_val=NP - P)
                                     for t in range(G)]
                        spread(g + 1, s + 1)
                        if k in (0, 1):
                            after(eng, f"mark_loaded_{s}", k, (it + 1) * 16)
                            vec.tensor_tensor(by_group(mark[:, s, :], TC)[:, :, 0:T],
                                              over_tiles(typ_f[:, ds(g * G, G)], T), over_lanes(iota[:, 0:T], G),
                                              ALU.is_equal).then_inc(q("marked"), 1)
                            hi1h = by_group(rank1h, NB)
                            one = vec.tensor_tensor(hi1h, over_lanes(iota[:, 0:NB], G),
                                                    over_tiles(src_hi[:, ds(g * G, G)], NB), ALU.is_equal)
                            if k == 0:
                                one.then_inc(q("rank_1h"), 1)
                            else:
                                st.did(one)
                                vec.tensor_tensor(by_group(rank_diag, NB),
                                                  over_lanes(w[0:NB, W_AT["ident"]:W_AT["ident"] + NB], G),
                                                  over_tiles(totals[:, ds(g * G, G)], NB), ALU.mult)\
                                   .then_inc(q("rank_diag"), 1)
                        if extra == "attr_by_src":
                            after(eng, "extra_used", k, g + 1)
                            st.did(vec.tensor_tensor(lane1h[:, s % 2, :, :], over_lanes(iota[:, 0:P], G),
                                                     over_tiles(src_lo[:, ds(g * G, G)], P), ALU.is_equal))
                            cols = by_group(big[:, s % 2, :], ST)
                            hi1h = cols[:, :, NB * A:MV]
                            st.do(vec.tensor_tensor(hi1h, over_lanes(iota[:, 0:NB], G),
                                                    over_tiles(src_hi[:, ds(g * G, G)], NB), ALU.is_equal))
                            attrs = by_group(mark[:, s, :], TC)[:, :, T:TC]
                            after(eng, f"mark_loaded_{s}", k, (it + 1) * 16)
                            vec.tensor_tensor(cols[:, :, 0:NB * A].rearrange("p k (b a) -> p k b a", a=A),
                                              hi1h.unsqueeze(3).to_broadcast([P, G, NB, A]),
                                              attrs.unsqueeze(2).to_broadcast([P, G, NB, A]),
                                              ALU.mult).then_inc(q("extra_ready"), 1)
                        if extra == "scatter":
                            after(eng, "extra_used", k, g + 1)
                            vec.tensor_tensor(lane1h[:, s % 2, :, :], over_lanes(iota[:, 0:P], G),
                                              over_tiles(slot_lane[:, ds(g * G, G)], P), ALU.is_equal)
                            for t in range(G):
                                last = vec.tensor_scalar(big[:, s % 2, t * ST:(t + 1) * ST], iota[:, 0:ST],
                                                         slot_tile[:, ds(g * G + t, 1)],
                                                         payload[:, ds(g * G + t, 1)], ALU.is_equal, ALU.mult)
                            last.then_inc(q("extra_ready"), 1)
                        after(eng, "summed", k, g + 1 + SUB)
                        for t, base in enumerate(bases):
                            n = len(bases)
                            out = ps[:, 2 * (s % 2) + t // 4, (t % 4) * P:(t % 4) * P + P] if n > 1 else ps[:, s % 2, 0:P]
                            after(eng, "added", k, g * n + t + 1)
                            vec.tensor_tensor(acc[:, ds(base, P)], acc[:, ds(base, P)], out, ALU.add)\
                               .then_inc(q("added"), 1)
                        if extra == "count":
                            eng.wait_ge(q("count_mm"), g + 1 + SUB)
                            eng.wait_ge(q("counted"), g + 1)
                            vec.tensor_tensor(nodes[DST_ROWS, ds(base, P)], nodes[DST_ROWS, ds(base, P)],
                                              ps[DST_ROWS, 2 + s % 2, 0:P], ALU.add).then_inc(q("counted"), 1)
                            eng.wait_ge(q("rank_mm"), g + 1)
                            st.do(vec.tensor_tensor(rank_prod, rank1h, ps[:, 4, 0:HW], ALU.mult))
                            st.did(vec.tensor_reduce(slot[:, ds(g * G, G)], by_group(rank_prod, NB), AX.X, ALU.add))
                            st.did(vec.tensor_copy(totals[:, ds(g * G, G)], ps[0:NB, 5, 0:G]))
                            st.settle()
                        if extra == "weigh":
                            eng.wait_ge(q("rank_base"), g + 1)
                            st.do(vec.tensor_tensor(rank_prod, rank1h, ps[:, 6, 0:HW], ALU.mult))
                            st.do(vec.tensor_reduce(flat[:, HPROD + 256:HPROD + 256 + G], by_group(rank_prod, NB),
                                                    AX.X, ALU.add))
                            vec.tensor_tensor(slot[:, ds(g * G, G)], slot[:, ds(g * G, G)],
                                              flat[:, HPROD + 256:HPROD + 256 + G], ALU.add)
                            eng.wait_ge(q("weigh_mm"), g + 2)
                            prod = by_group(flat[:, PROD:PROD + GE], P)
                            st.do(vec.tensor_tensor(prod, onehot[:, s % 2, :, :], by_group(psf[:, 2048:2048 + GE], P),
                                                    ALU.mult))
                            vec.tensor_reduce(edge_w[:, ds(g * G, G)], prod, AX.X, ALU.add).then_inc(q("weighed"), 1)
                            eng.wait_ge(q("weighed"), g + 2)
                    st.leave(passes)
                after(eng, "added", k, 1 + last_group * (G if k == BY_SRC else 1))
                if extra == "count":
                    eng.wait_ge(q("counted"), 1 + NG)
                if k < 2:
                    vec.engine_nop().then_inc(q("loop_done"), 1)

            def block_starts():
                st.do(vec.tensor_tensor_scan(scanned, totals, totals, 0.0, ALU.add, ALU.bypass))
                st.do(vec.tensor_scalar(blk[:, 0:1], scanned[:, NT - 1:NT], float(P - 1), None, ALU.add))
                st.do(vec.tensor_copy(blk_i[:, 0:1], blk[:, 0:1]))
                st.do(vec.tensor_scalar(blk_i[:, 1:2], blk_i[:, 0:1], -P, None, ALU.bitwise_and))
                vec.tensor_copy(blk[:, 1:2], blk_i[:, 1:2]).then_inc(q("block_size"), 1)
                eng.wait_ge(q("block_start"), 1)
                st.did(vec.tensor_tensor(blk[:, 3:4], ps[0:NB, 6, 0:1], blk[:, 1:2], ALU.add))
                st.did(vec.tensor_tensor(totals, scanned, totals, ALU.subtract))
                st.settle()
                st.do(vec.tensor_scalar(totals, totals, ps[0:NB, 6, 0:1], None, ALU.add))
                st.do(vec.tensor_scalar(flat[0:NB, HDIAG:HDIAG + ST], iota[0:NB, 0:ST], float(P), None, ALU.mult))
                vec.tensor_scalar(flat[0:NB, HI1H:HI1H + ST], flat[0:NB, HDIAG:HDIAG + ST], blk[:, 3:4], None,
                                  ALU.is_ge).then_inc(q("block_ended"), 1)
                eng.wait_ge(q("tile_block"), 1)
                st.do(vec.tensor_scalar(gcn_base[:], ps[:, 7, 0:ST], float(P), float(NP - P), ALU.mult, ALU.min))

            def degrees():
                st.do(vec.tensor_copy(by_src[:], ps[:, 7, 0:MV]))
                st.did(vec.tensor_scalar(deg[:, 2, :], by_src[:, NB * A:MV], 0.0, None, ALU.is_gt))
                vec.tensor_scalar(deg[:, 0, :], by_src[:, NB * A:MV], 1.0, None, ALU.max).then_inc(q("degree"), 1)
                eng.wait_ge(q("degree"), 1)
                st.did(vec.reciprocal(deg[:, 3, :], deg[:, 0, :]))
                eng.wait_ge(q("deg_sqrt"), 1)
                st.do(vec.reciprocal(dinv[:], deg[:, 1, :]))
                st.do(vec.tensor_tensor(dinv[:], dinv[:], deg[:, 2, :], ALU.mult))
                sums = by_group(by_src[:, 0:NB * A], A)
                st.do(vec.tensor_tensor(sums, sums, over_tiles(deg[:, 3, :], A), ALU.mult))

            def slots():
                st.do(vec.tensor_copy(slot_i[:], slot[:]))
                st.did(vec.tensor_scalar(src[:], slot_i[:], P - 1, None, ALU.bitwise_and))
                st.did(vec.tensor_scalar(dst[:], slot_i[:], 7, None, ALU.arith_shift_right))
                st.settle()
                st.did(vec.tensor_copy(slot_lane[:], src[:]))
                st.do(vec.tensor_copy(slot_tile[:], dst[:]))

            def sender_order():
                whole = flat[:, HI1H:HI1H + ST].bitcast(I32)
                st.do(vec.tensor_copy(whole, ps[:, 7, 0:ST]))
                st.did(vec.tensor_scalar(gcn_idx[:], whole, 4095, None, ALU.bitwise_and))
                high = flat[:, HDIAG:HDIAG + ST].bitcast(I32)
                st.do(vec.tensor_scalar(high, whole, 12, None, ALU.arith_shift_right))
                st.do(vec.tensor_scalar(gcn_lo[:, 0:ST], high, -1.0, None, ALU.add))

            def gru(l, i, between=lambda some: None):
                if i >= NCH:
                    between(slice(None))
                    return
                n = width(i)
                r, z, cand, new = tmp[:, 2 + i % 2, 0:n], tmp[:, 4 + i % 2, 0:n], tmp[:, 6, 0:n], tmp[:, 7, 0:n]
                after(eng, "gru_rz", l, i + 1)
                st.do(vec.scalar_tensor_tensor(out=cand, in0=bank(7, i), scalar=bs(f"bhh{l}_n"), in1=r,
                                               op0=ALU.add, op1=ALU.mult))
                vec.tensor_tensor(cand, cand, bank(6, i), ALU.add).then_inc(q("gru_cand"), 1)
                between(slice(0, 1))
                after(eng, "gru_n", l, i + 1)
                if i >= 1:
                    after(eng, "gru_h", l, i)
                st.do(vec.tensor_tensor(new, chunk(h, i), cand, ALU.subtract))
                st.do(vec.tensor_tensor(new, new, z, ALU.mult))
                vec.tensor_tensor(new, new, cand, ALU.add).then_inc(q("gru_mixed"), 1)
                between(slice(1, None))
                after(eng, "gru_mixed", l, i + 1)

            def normalize(c, centered, sd, done):
                st.do(vec.reciprocal(sd, sd))
                vec.tensor_tensor(chunk(x, c), centered, sd, ALU.mult).then_inc(q(done), 1)

            prep()
            for c in range(NCH):
                table(0, c)
            windows()
            edge_sums(0)
            for i in range(NCH + 1):
                gru(0, i, lambda some: table(1, i - 1, some))
            st.do(vec.tensor_scalar(nodes[INV_ROWS, :], nodes[32:32 + T, :], 1.0, None, ALU.max))
            vec.reciprocal(nodes[INV_ROWS, :], nodes[INV_ROWS, :]).then_inc(q("inv_ready"), 1)
            block_starts()
            edge_sums(1)
            for i in range(NCH + 3):
                gru(1, i)
                if 1 <= i < NCH + 1:
                    c = i - 1
                    eng.wait_ge(q("out_mm"), c + 1)
                    vec.scalar_tensor_tensor(out=chunk(acc, c), in0=bank(3, c), scalar=bs("out"), in1=chunk(x, c),
                                             op0=ALU.add, op1=ALU.add).then_inc(q("ln_in"), 1)
                if 2 <= i < NCH + 2:
                    c = i - 2
                    after(eng, "ln_sq", 0, c + 1)
                    vec.tensor_copy(chunk(acc, c), bank(0, c)).then_inc(q("ln_kept"), 1)
            eng.wait_ge(q("ln_kept"), NCH)
            for i in range(NCH + 1):
                if i < NCH:
                    after(eng, "ln_sd", 0, i + 1)
                    normalize(i, chunk(acc, i), tmp[:, 2 + i % 2, 0:width(i)], "ln_out")
                table(2, i - 1)
            edge_sums(2)
            for k in (3, 4):
                for i in range(NCH + 1):
                    if i < NCH:
                        vec.scalar_tensor_tensor(out=chunk(h, i), in0=chunk(acc, i), scalar=0.0, in1=chunk(res, i),
                                                 op0=ALU.max, op1=ALU.add).then_inc(q("h_ready"), 1)
                    table(k, i - 1)
                if k == 3:
                    degrees()
                    slots()
                else:
                    sender_order()
                edge_sums(k)
            for i in range(NCH + 2):
                if i < NCH:
                    st.do(vec.scalar_tensor_tensor(out=chunk(h, i), in0=chunk(acc, i), scalar=0.0, in1=chunk(res, i),
                                                   op0=ALU.max, op1=ALU.add))
                    vec.tensor_tensor(chunk(acc, i), chunk(h, i), chunk(x, i), ALU.add).then_inc(q("ln_in"), 1)
                if 1 <= i < NCH + 1:
                    c = i - 1
                    after(eng, "ln_sd", 1, c + 1)
                    normalize(c, bank(c % 2, c), tmp[:, 2 + c % 2, 0:width(c)], "ln_out")
                if i >= 2:
                    c = i - 2
                    n = len(blocks_of(c))
                    eng.wait_ge(q("gcn_mm"), c + 1)
                    vec.tensor_tensor(by_group(chunk(flat, c), P), by_group(bank(4 + c % 2, c), P),
                                      over_tiles(dinv[:, c * CB:c * CB + n], P), ALU.mult).then_inc(q("gcn_rows"), 1)
            for c in range(NCH):
                eng.wait_ge(q("dst_count_mm"), c + 1)
                inv = tmp[:, c % 2, 0:width(c)]
                st.do(vec.tensor_scalar(inv, bank(4 + c % 2, c), 1.0, None, ALU.max))
                st.do(vec.reciprocal(inv, inv))
                vec.tensor_tensor(chunk(nodes, c), chunk(nodes, c), inv, ALU.mult).then_inc(q("by_dst_mean"), 1)
                eng.wait_ge(q("by_dst_mean"), c + 1)
            edge_sums(BY_SRC)
            for i in range(NCH + 6):
                if i < NCH:
                    st.do(vec.tensor_tensor(chunk(acc, i), chunk(acc, i), chunk(res, i), ALU.mult))
                    vec.scalar_tensor_tensor(out=chunk(acc, i), in0=chunk(acc, i), scalar=bs("gcn"), in1=chunk(x, i),
                                             op0=ALU.add, op1=ALU.add).then_inc(q("n2_in"), 1)
                if 1 <= i < NCH + 1:
                    c = i - 1
                    eng.wait_ge(q("n2_sd"), c + 1)
                    normalize(c, bank(6 * (c % 2), c), tmp[:, 1, 0:width(c)], "n2_out")
                if 2 <= i < NCH + 2:
                    c = i - 2
                    eng.wait_ge(q("mlp_pre"), c + 1)
                    if c >= 1:
                        eng.wait_ge(q("mlp2_mm"), c)
                    vec.scalar_tensor_tensor(out=tmp[:, 3, 0:width(c)], in0=tmp[:, 2, 0:width(c)], scalar=0.01,
                                             in1=tmp[:, 2, 0:width(c)], op0=ALU.mult, op1=ALU.max)\
                       .then_inc(q("mlp_hidden"), 1)
                if 3 <= i < NCH + 3:
                    c = i - 3
                    eng.wait_ge(q("mlp2_mm"), c + 1)
                    vec.scalar_tensor_tensor(out=chunk(acc, c), in0=bank(3, c), scalar=bs("mlp2"), in1=chunk(x, c),
                                             op0=ALU.add, op1=ALU.add).then_inc(q("n3_in"), 1)
                if 5 <= i < NCH + 5:
                    c = i - 5
                    eng.wait_ge(q("n3_sd"), c + 1)
                    normalize(c, bank(4 + 3 * (c % 2), c), tmp[:, 5, 0:width(c)], "n3_out")


def _layout(v):
    f32 = np.float32

    def tiles(a, fill):
        full = np.full((NT * P,) + a.shape[1:], fill, a.dtype)
        full[:EDGES] = a
        return full

    def lanes(a):
        return np.ascontiguousarray(tiles(a, NONE).reshape(NT, P).T)

    blocks = {"proj": v["L0_gnn_node_proj_w"].T, "out": v["L0_gnn_out_w"].T, "res": v["L1_gnn_res_w"],
              "gcn": v["L2_gnn_W"].T, "w1x": v["L3_gnn_W1"][:P], "w2": v["L3_gnn_W2"]}
    cols = {"proj": v["L0_gnn_node_proj_b"], "out": v["L0_gnn_out_b"], "res": v["L1_gnn_res_b"],
            "gcn": v["L2_gnn_b"], "mlp1": v["L3_gnn_b1"], "mlp2": v["L3_gnn_b2"], "eps": np.full(P, EPS, f32)}
    for l in range(2):
        for t in range(T):
            blocks[f"edge{l}_{t}"] = v["L0_gnn_edge_W"][l, t].T
        for i, g in enumerate("rzn"):
            part = slice(i * P, (i + 1) * P)
            blocks[f"wih{l}_{g}"] = v["L0_gnn_gru_wih"][l, part].T
            blocks[f"whh{l}_{g}"] = v["L0_gnn_gru_whh"][l, part].T
            cols[f"bih{l}_{g}"] = v["L0_gnn_gru_bih"][l, part]
            cols[f"bhh{l}_{g}"] = v["L0_gnn_gru_bhh"][l, part]
    for l in range(3):
        for t in range(T):
            blocks[f"rel{l}_{t}"] = v[f"L1_gnn_W{l + 1}"][t]
        blocks[f"root{l}"] = v[f"L1_gnn_root{l + 1}"]
        cols[f"b{l}"] = v[f"L1_gnn_b{l + 1}"]
    w1a = np.zeros((P, P), f32)
    w1a[SRC_ROWS] = v["L3_gnn_W1"][P:P + A]
    w1a[DST_ROWS.start + T:DST_ROWS.stop] = v["L3_gnn_W1"][P + A:]
    blocks["w1a"] = w1a
    blocks["ident"] = np.eye(P, dtype=f32)
    blocks["mean"] = np.full((P, P), 1 / P, f32)
    blocks["center"] = np.eye(P, dtype=f32) - np.full((P, P), 1 / P, f32)
    blocks["before"] = np.triu(np.ones((P, P), f32), 1)
    blocks["ones"] = np.ones((P, P), f32)
    count = np.zeros((P, P), f32)
    count[DST_ROWS.start:DST_ROWS.start + T, DST_ROWS] = 1
    blocks["dst_count"] = count

    xT = np.zeros((P, NV), f32)
    xT[:, :NODES] = v["x"].T
    marks = np.zeros((NT * P, TC), f32)
    marks[:EDGES, T:] = v["edge_attr_16"]
    zero = np.zeros(P, f32)
    return {
        "xT": xT, "dst_rows": tiles(v["dst"], NONE).reshape(NG, GE), "dst_lanes": lanes(v["dst"]),
        "src_lanes": lanes(v["src"]), "typ_lanes": lanes(v["edge_type_8"]),
        "marks": np.ascontiguousarray(marks.reshape(NT, P, TC).transpose(1, 0, 2)).reshape(P, NT * TC),
        "weights": np.ascontiguousarray(np.concatenate([blocks[n] for n in W_NAMES], axis=1)),
        "biases": np.ascontiguousarray(np.stack([cols.get(n, zero) for n in B_NAMES], axis=1)),
        "iota": np.ascontiguousarray(np.broadcast_to(np.arange(512, dtype=f32), (P, 512))),
    }


def kernel(**inputs):
    import concourse.bacc as _bacc
    from concourse.bass_utils import run_bass_kernel_spmd as _run

    nc = _bacc.Bacc("TRN2", target_bir_lowering=False, num_devices=1)
    arrays = _layout({k: np.asarray(a) for k, a in inputs.items()})
    args = [nc.dram_tensor(f"in_{n}", a.shape, mybir.dt.from_np(a.dtype), kind="ExternalInput").ap()
            for n, a in arrays.items()]
    args.append(nc.dram_tensor("out_0", (P, NV), F32, kind="ExternalOutput").ap())
    graph_kernel(nc, *args)
    r = _run(nc, [{f"in_{n}": a for n, a in arrays.items()}], core_ids=[0])
    return np.ascontiguousarray(r.results[0]["out_0"][:, :NODES].T)
```

```python
from contextlib import ExitStack

import numpy as np
import concourse.bass as bass
from concourse import mybir

F32 = mybir.dt.float32
I32 = mybir.dt.int32
ALU = mybir.AluOpType
ACT = mybir.ActivationFunctionType
AX = mybir.AxisListType
ds = bass.ds

P = 128
NODES = 3125
EDGES = 53125
NB = 26
NP = NB * P
TB = 25
NV = TB * P
CB = 4
CH = CB * P
NCH = -(-TB // CB)
SLOTS = 4
T = 8
A = 16
TC = T + A
G = 8
GE = G * P
NG = -(-EDGES // GE)
NT = NG * G
SUB = 4
PASSES = NG // SUB
AHEAD = 2
NONE = 8191
HW = G * NB
MV = NB * A + NB
ST = 448
SPASSES = ST // (SUB * G)
EPS = 1e-5
assert NG % SUB == 0 and NODES <= NV and NODES + P <= NP and MV <= 512
assert ST % (SUB * G) == 0 and ST * P >= EDGES + NB * (P - 1)

W_NAMES = (["proj"] + [f"edge0_{t}" for t in range(T)] + ["ident", "ones", "before"]
           + [f"edge1_{t}" for t in range(T)]
           + [f"{s}{l}_{g}" for l in range(2) for s in ("wih", "whh") for g in "rzn"] + ["out", "res"]
           + [f"rel{l}_{t}" for l in range(3) for t in range(T)] + [f"root{l}" for l in range(3)]
           + ["gcn", "w1x", "w1a", "w2", "center", "mean"])
W_FIRST = 4 + T
W_AT = {n: i * P for i, n in enumerate(W_NAMES)}
B_NAMES = (["proj"] + [f"{s}{l}_{g}" for l in range(2) for s in ("bih", "bhh") for g in "rzn"]
           + [f"both{l}_{g}" for l in range(2) for g in "rz"]
           + ["out", "res", "b0", "b1", "b2", "gcn", "mlp1", "mlp2", "eps"])
B_AT = {n: i for i, n in enumerate(B_NAMES)}
COUNT_ROWS, DST_ROWS, SRC_ROWS = slice(0, T), slice(32, 32 + TC), slice(64, 64 + A)


class Steps:

    def __init__(self, eng, sem):
        self.eng, self.sem, self.base, self.j = eng, sem, 0, 0

    def did(self, ins):
        ins.then_inc(self.sem, 1)
        self.j += 1

    def settle(self):
        self.eng.wait_ge(self.sem, self.base + self.j)

    def do(self, ins):
        self.did(ins)
        self.settle()

    def enter(self, it, step):
        self.start, self.step, self.base, self.j = self.base + self.j, step, self.base + self.j + it * step, 0

    def leave(self, passes):
        assert self.j == self.step, self.j
        self.base, self.j = self.start + passes * self.step, 0


TOTALS = {
    "tab_mm": TB, "tab_act": TB, "tab_dve": TB, "h_ready": NCH, "root_mm": NCH, "root_used": NCH,
    "summed": SUB + NG, "onehot": 1 + NG, "added": 1 + NG, "gathered": 16 * G * PASSES, "idx_staged": NG,
    "marked": NG, "lane_ready": NG, "mark_loaded": 16 * PASSES, "zeros": 1, "opened": 1,
    "extra_ready": SUB + NG, "extra_used": 2 + NG, "state_mm": NCH, "state_kept": NCH, "gru_mm": NCH,
    "gru_rz": NCH, "gru_cand": NCH, "gru_n": NCH, "gru_mixed": NCH, "gru_h": NCH,
    "ln_in": NCH, "ln_center": NCH, "ln_sq": NCH, "ln_kept": NCH, "ln_var": NCH, "ln_sd": 1, "ln_rstd": 1,
    "ln_spread": NCH, "ln_out": NCH,
}
FIRST_RUN = {"lane_ready": 2, "zeros": 2, "opened": 2, "extra_ready": 2, "extra_used": 2, "root_mm": 2,
             "root_used": 2}


def graph_kernel(nc, xT_d, dst_rows_d, dst_d, src_d, typ_d, mark_d, w_d, b_d, iota_d, out_d):
    with ExitStack() as ctx:
        def sb(name, shape, dt=F32):
            return ctx.enter_context(nc.sbuf_tensor(name, shape, dt))

        sems = {}

        def q(name):
            if name not in sems:
                sems[name] = ctx.enter_context(nc.semaphore(name))
            return sems[name]

        def after(eng, name, run, count):
            kind = name.rsplit("_", 1)[0] if name[-1].isdigit() else name
            eng.wait_ge(q(name), TOTALS[kind] * (run - FIRST_RUN.get(kind, 0)) + count)

        def stored(eng, k, b):
            s = b % SLOTS
            eng.wait_ge(q(f"table_stored_{s}"), 16 * (k * len(range(s, TB, SLOTS)) + b // SLOTS + 1))

        def all_stored(eng, k):
            for b in range(TB - SLOTS, TB):
                stored(eng, k, b)

        table_d = nc.dram_tensor("messages", (NV, T * P), F32).ap()
        gcn_table_d = nc.dram_tensor("gcn_rows", (NV, P), F32).ap()
        table_rows = table_d.rearrange("n (t d) -> (n t) d", t=T)

        ps = ctx.enter_context(nc.psum_tensor("ps", [P, 8, 512], F32))
        psf = ps[:].rearrange("p a b -> p (a b)")

        w = sb("w", [P, len(W_NAMES) * P])
        bias = sb("bias", [P, len(B_NAMES)])
        iota = sb("iota", [P, 512])
        x = sb("x", [P, NV])
        h = sb("h", [P, NV])
        res = sb("res", [P, NV])
        acc = sb("acc", [P, NP])
        nodes = sb("nodes", [P, NP])
        dst = sb("dst", [P, NT], I32)
        src = sb("src", [P, NT], I32)
        typ = sb("typ", [P, NT], I32)
        row_idx = sb("row_idx", [P, NT + AHEAD * G], I32)
        dst_lo = sb("dst_lo", [P, NT + G])
        src_lo = sb("src_lo", [P, NT])
        src_hi = sb("src_hi", [P, NT + G])
        typ_f = sb("typ_f", [P, NT + G])
        edge_w = sb("edge_w", [P, NT + G])
        base_f = sb("base_f", [P, NG])
        base_i = sb("base_i", [P, NG], I32)
        base_diag = sb("base_diag", [NG, NG])
        first = sb("first", [NG, 1])
        far_any = sb("far_any", [P, 1])
        far_flag = sb("far_flag", [P, 1], I32)
        far_lo = sb("far_lo", [P, G])
        far_w = sb("far_w", [P, G])
        msg = sb("msg", [P, SUB, G, P])
        mark = sb("mark", [P, SUB, G * TC])
        idx_buf = sb("idx_buf", [P, SUB, G], I32)
        onehot = sb("onehot", [P, 2, G, P])
        lane1h = sb("lane1h", [P, 2, G, P])
        big = sb("big", [P, 2, G * ST])
        gcn_idx = sb("gcn_idx", [P, ST], I32)
        gcn_lo = sb("gcn_lo", [P, ST + G])
        gcn_base = sb("gcn_base", [P, ST], I32)
        slot = sb("slot", [P, NT])
        payload = sb("payload", [P, NT])
        by_src = sb("by_src", [P, MV])
        deg = sb("deg", [P, 4, NB])
        stat = sb("stat", [P, 2, TB])
        dinv = sb("dinv", [P, NB])
        blk = sb("blk", [NB, 4])
        blk_i = sb("blk_i", [NB, 2], I32)
        tmp = sb("tmp", [P, 8, CH])
        flat = big[:].rearrange("p a b -> p (a b)")
        slot_i, slot_tile, slot_lane, valid = typ, typ_f[:, 0:NT], src_hi[:, 0:NT], edge_w[:, 0:NT]
        spare = lane1h[0:NB, 1, :, :].rearrange("p a b -> p (a b)")
        totals, scanned = spare[:, 0:NT + G], spare[:, 512:512 + NT]
        TT, PROD, HI1H, HPROD, HDIAG = 0, GE, 4096, 4608, 5120
        rank1h = [flat[:, HI1H + i * 256:HI1H + i * 256 + HW] for i in range(2)]
        rank_prod = flat[:, HPROD:HPROD + HW]
        rank_diag = [flat[0:NB, HDIAG + i * 256:HDIAG + i * 256 + HW] for i in range(2)]

        def wt(name, n=1):
            return w[:, W_AT[name]:W_AT[name] + n * P]

        def bs(name):
            return bias[:, B_AT[name]:B_AT[name] + 1]

        def width(c):
            return min(CH, NV - c * CH)

        def chunk(buf, c):
            return buf[:, c * CH:c * CH + width(c)]

        def bank(i, c):
            return ps[:, i, 0:width(c)]

        def blocks_of(c):
            return range(c * CB, min(c * CB + CB, TB))

        def block_of(buf, b):
            return buf[:, b * P:(b + 1) * P]

        def by_group(buf, cols):
            return buf.rearrange("p (k c) -> p k c", c=cols)

        loops = [
            (row_idx, dst_lo, False, table_rows, PASSES, "count"),
            (row_idx, dst_lo, False, table_rows, PASSES, "weigh"),
            (row_idx, dst_lo, True, table_rows, PASSES, "attr_by_src"),
            (row_idx, dst_lo, True, table_rows, PASSES, "scatter"),
            (row_idx, dst_lo, True, table_rows, PASSES, None),
            (gcn_idx, gcn_lo, False, gcn_table_d, SPASSES, None),
        ]
        mark_free = {0: "count_mm", 2: "extra_ready"}
        BY_SRC = 5
        FAR_GROUPS, FAR_STEPS = 1 + NG, NG * TB

        block = ctx.enter_context(nc.Block())

        @block.sync
        def _(eng):
            eng.dma_start(bias[:], b_d).then_inc(q("loaded_x"), 16)
            eng.dma_start(w[:, 0:P], w_d[:, 0:P]).then_inc(q("loaded_x"), 16)
            eng.dma_start(x[:], xT_d).then_inc(q("loaded_x"), 16)
            eng.dma_start(w[:, P:W_FIRST * P], w_d[:, P:W_FIRST * P]).then_inc(q("loaded_w"), 16)
            eng.dma_start(flat[0:NG, 6144:6144 + GE].bitcast(I32), dst_rows_d).then_inc(q("loaded"), 16)
            for buf, d in ((dst, dst_d), (src, src_d), (typ, typ_d), (iota, iota_d)):
                eng.dma_start(buf[:], d).then_inc(q("loaded"), 16)
            eng.dma_start(w[:, W_FIRST * P:], w_d[:, W_FIRST * P:]).then_inc(q("loaded_rest"), 16)

            for k in range(5):
                for b in range(TB):
                    s = b % SLOTS
                    after(eng, "tab_act", k, b + 1)
                    after(eng, "tab_dve", k, b + 1)
                    eng.dma_start(table_d[b * P:(b + 1) * P, :], flat[:, s * 1024:(s + 1) * 1024])\
                       .then_inc(q(f"table_stored_{s}"), 16)
                if k in mark_free:
                    with eng.Fori(0, PASSES) as it:
                        for s in range(SUB):
                            eng.wait_ge(q(mark_free[k]), it * SUB + s + 1)
                            eng.dma_start(mark[:, s, :], mark_d[:, ds((it * SUB + s) * (G * TC), G * TC)])\
                               .then_inc(q(f"mark_loaded_{s}"), 16)
                if k == 0:
                    eng.wait_ge(q("far_known"), 1)
                    with eng.If(eng.value_load(far_flag[0:1, 0:1], min_val=0, max_val=1) > 0):
                        with eng.Fori(0, NG) as g:
                            eng.wait_ge(q("far_free"), g + 1)
                            eng.dma_start(mark[:, 0, :], mark_d[:, ds(g * (G * TC), G * TC)])\
                               .then_inc(q("far_marks"), 16)
            for c in range(NCH):
                n = len(blocks_of(c))
                eng.wait_ge(q("gcn_rows"), c + 1)
                eng.dma_start(gcn_table_d[c * CH:c * CH + width(c), :].rearrange("(b p) d -> p b d", p=P),
                              chunk(flat, c).rearrange("p (b d) -> p b d", d=P)).then_inc(q("gcn_stored"), 16)
            for c in range(NCH):
                after(eng, "ln_out", 3, c + 1)
                eng.dma_start(chunk(out_d, c), chunk(x, c)).then_inc(q("out_stored"), 16)
            eng.wait_ge(q("out_stored"), 16 * NCH)

        @block.gpsimd
        def _(eng):
            def far(k, idx):
                if k == 0:
                    eng.wait_ge(q("far_known"), 1)
                with eng.If(eng.value_load(far_flag[0:1, 0:1], min_val=0, max_val=1) > 0):
                    with eng.Fori(0, NG) as g:
                        eng.wait_ge(q("far_free"), g + (1 + k * FAR_GROUPS))
                        eng.tensor_copy(idx_buf[:, 0, :], idx[:, ds(g * G, G)]).then_inc(q("far_idx"), 1)
                        eng.wait_ge(q("far_idx"), g + (1 + k * NG))
                        eng.sem_inc(q("rows_known"), 1)
                        for t in range(G):
                            eng.indirect_dma_start(msg[:, 0, t, :], None, table_rows,
                                                   bass.IndirectOffsetOnAxis(ap=idx_buf[:, 0, t:t + 1], axis=0))\
                               .then_inc(q("far_gathered"), 16)

            for k, (idx, lo, weighted, table, passes, extra) in enumerate(loops):
                if k == 0:
                    eng.wait_ge(q("rows_ready"), 1)
                if k == BY_SRC:
                    eng.wait_ge(q("gcn_stored"), 16 * NCH)
                else:
                    all_stored(eng, k)
                with eng.Fori(0, passes) as it:
                    for s in range(SUB):
                        after(eng, "idx_staged", k, it * SUB + s + (1 + AHEAD * min(max(k - 1, 0), 3)))
                        eng.sem_inc(q("rows_known"), 1)
                        for t in range(G):
                            eng.indirect_dma_start(msg[:, s, t, :], None, table,
                                                   bass.IndirectOffsetOnAxis(ap=idx_buf[:, s, t:t + 1], axis=0))\
                               .then_inc(q(f"gathered_{s}"), 16)
                if k != BY_SRC:
                    far(k, idx)

        @block.tensor
        def _(eng):
            mm = eng.matmul

            def table(k, weight, source, c):
                for b in blocks_of(c):
                    p = b % 2
                    if b >= 2:
                        after(eng, "tab_act", k, b - 1)
                        after(eng, "tab_dve", k, b - 1)
                    mm(ps[:, 2 * p, :], block_of(source, b), wt(weight, T)[:, 0:512], start=True, stop=True)
                    mm(ps[:, 2 * p + 1, :], block_of(source, b), wt(weight, T)[:, 512:1024], start=True, stop=True)\
                        .then_inc(q("tab_mm"), 1)

            def edge_sums(k):
                idx, lo, weighted, tab, passes, extra = loops[k]
                wide = extra in ("attr_by_src", "scatter")
                n = MV if extra == "attr_by_src" else ST
                if extra == "count":
                    eng.sem_inc(q("count_mm"), SUB)
                if extra == "weigh":
                    eng.sem_inc(q("weigh_mm"), 1)
                    eng.wait_ge(q("counts_ready"), 1)
                if wide:
                    after(eng, "zeros", k, 1)
                    mm(ps[:, 7, 0:n], wt("ones"), flat[:, G * ST:G * ST + n], start=True, stop=False,
                       skip_group_check=True).then_inc(q("opened"), 1)
                    eng.sem_inc(q("extra_used"), 2)
                if k == BY_SRC:
                    eng.wait_ge(q("by_dst_mean"), NCH)
                    after(eng, "zeros", 4, 1)
                    for c in range(NCH):
                        mm(ps[:, c, :], wt("ones"), flat[:, G * ST:G * ST + 512], start=True, stop=False,
                           skip_group_check=True)
                with eng.Fori(0, passes) as it:
                    for s in range(SUB):
                        g = it * SUB + s
                        if k == BY_SRC:
                            bases = [eng.value_load(gcn_base[0:1, ds(g * G + t, 1)], min_val=0, max_val=NP - P)
                                     for t in range(G)]
                        if extra == "weigh":
                            base = eng.value_load(base_i[0:1, ds(g, 1)], min_val=0, max_val=NP - P)
                            after(eng, "marked", 1, g + 1)
                            for t in range(G):
                                last = mm(ps[0:T, 2 + t // 4, (t % 4) * P:(t % 4) * P + P],
                                          mark[:, s, t * TC:t * TC + T], wt("ident"), start=True, stop=True)
                            last.then_inc(q("turned"), 1)
                            eng.wait_ge(q("rank_diag"), g + 1)
                            mm(ps[:, 6 + s % 2, 0:HW], w[0:NB, W_AT["ones"]:W_AT["ones"] + P], rank_diag[s % 2],
                               start=True, stop=True).then_inc(q("rank_base"), 1)
                        after(eng, "onehot", k, g + 1)
                        after(eng, f"gathered_{s}", k, (it + 1) * (16 * G))
                        for t in range(G):
                            if k == BY_SRC:
                                last = mm(psf[:, ds(bases[t], P)], msg[:, s, t, :], onehot[:, s % 2, t, :],
                                          start=False, stop=False, skip_group_check=True)
                            else:
                                last = mm(ps[:, s % 2, 0:P], msg[:, s, t, :], onehot[:, s % 2, t, :],
                                          start=t == 0, stop=t == G - 1)
                        last.then_inc(q("summed"), 1)
                        if extra == "count":
                            eng.wait_ge(q("marked"), g + 1)
                            for t in range(G):
                                last = mm(ps[DST_ROWS, 2 + s % 2, 0:P], mark[:, s, t * TC:(t + 1) * TC],
                                          onehot[:, s % 2, t, :], start=t == 0, stop=t == G - 1)
                            last.then_inc(q("count_mm"), 1)
                            eng.wait_ge(q("rank_1h"), g + 1)
                            for t in range(G):
                                mm(ps[0:NB, 5, t:t + 1], rank1h[0][:, t * NB:(t + 1) * NB], wt("ones")[:, 0:1],
                                   start=True, stop=True)
                            mm(ps[:, 4, 0:HW], wt("before"), rank1h[0], start=True, stop=True).then_inc(q("rank_mm"), 1)
                        if extra == "weigh":
                            eng.wait_ge(q("turned_copied"), g + 1)
                            eng.wait_ge(q("weighed"), g + 1)
                            for t in range(G):
                                last = mm(ps[:, 4 + t // 4, (t % 4) * P:(t % 4) * P + P],
                                          flat[COUNT_ROWS, TT + t * P:TT + (t + 1) * P], nodes[COUNT_ROWS, ds(base, P)],
                                          start=True, stop=True)
                            last.then_inc(q("weigh_mm"), 1)
                        if wide:
                            after(eng, "extra_ready", k, g + 1 + SUB * (k == 2))
                            after(eng, "lane_ready", k, g + 1)
                            for t in range(G):
                                last = mm(ps[:, 7, 0:n], lane1h[:, s % 2, t, :], big[:, s % 2, t * ST:t * ST + n],
                                          start=False, stop=False, skip_group_check=True)
                            last.then_inc(q("extra_used"), 1)

            def far(k):
                with eng.If(eng.value_load(far_flag[0:1, 0:1], min_val=0, max_val=1) > 0):
                    with eng.Fori(0, NG) as g:
                        with eng.Fori(0, TB) as b:
                            step = g * TB + b
                            eng.wait_ge(q("far_gathered"), (g + (1 + k * NG)) * (16 * G))
                            if k == 1:
                                eng.wait_ge(q("far_types"), step + (1 + FAR_STEPS))
                                for t in range(G):
                                    last = mm(ps[0:T, 2 + t // 4, (t % 4) * P:(t % 4) * P + P],
                                              mark[:, 0, t * TC:t * TC + T], wt("ident"), start=True, stop=True)
                                last.then_inc(q("far_turned"), 1)
                            eng.wait_ge(q("far_onehot"), step + (1 + k * FAR_STEPS))
                            if k == 1:
                                eng.wait_ge(q("far_copied"), step + 1)
                            for t in range(G):
                                last = mm(ps[:, 0, 0:P], msg[:, 0, t, :], onehot[:, 0, t, :], start=t == 0,
                                          stop=t == G - 1)
                            if k == 0:
                                for t in range(G):
                                    last = mm(ps[DST_ROWS, 2, 0:P], mark[:, 0, t * TC:(t + 1) * TC],
                                              onehot[:, 0, t, :], start=t == 0, stop=t == G - 1)
                            if k == 1:
                                for t in range(G):
                                    last = mm(ps[:, 4 + t // 4, (t % 4) * P:(t % 4) * P + P],
                                              flat[COUNT_ROWS, TT + t * P:TT + (t + 1) * P],
                                              nodes[COUNT_ROWS, ds(b * P, P)], start=True, stop=True)
                            last.then_inc(q("far_mm"), 1)

            def gru(l, c):
                if c >= 1:
                    after(eng, "gru_rz", l, c)
                    after(eng, "gru_cand", l, c)
                for i, gate in enumerate("rz"):
                    mm(bank(4 + i, c), wt(f"wih{l}_{gate}"), chunk(acc, c), start=True, stop=False)
                    mm(bank(4 + i, c), wt(f"whh{l}_{gate}"), chunk(h, c), start=False, stop=True)
                mm(bank(6, c), wt(f"wih{l}_n"), chunk(acc, c), start=True, stop=True).then_inc(q("gru_mm"), 1)

            def candidate_state(l):
                for c in range(NCH):
                    if c >= 2:
                        after(eng, "state_kept", l, c - 1)
                    mm(bank(4 + c % 2, c), wt(f"whh{l}_n"), chunk(h, c), start=True, stop=True)\
                        .then_inc(q("state_mm"), 1)
                after(eng, "state_kept", l, NCH)

            def open_rows():
                eng.sem_inc(q("summed"), SUB)

            def ln_center(r, c, bank_no):
                if c >= 2:
                    after(eng, "ln_kept", r, c - 1)
                mm(bank(bank_no, c), wt("center"), chunk(acc, c), start=True, stop=True).then_inc(q("ln_center"), 1)

            def ln_var(r, c, bank_no):
                after(eng, "ln_sq", r, c + 1)
                for b in blocks_of(c):
                    last = mm(ps[:, bank_no, b:b + 1], tmp[:, c % 2, (b % CB) * P:(b % CB + 1) * P],
                              wt("mean")[:, 0:1], start=True, stop=True)
                last.then_inc(q("ln_var"), 1)

            def ln_spread(r, c, bank_no):
                after(eng, "ln_rstd", r, 1)
                if c >= 2:
                    after(eng, "ln_out", r, c - 1)
                for b in blocks_of(c):
                    last = mm(ps[:, bank_no, (b % CB) * P:(b % CB + 1) * P], stat[:, 1, b:b + 1].to_broadcast([P, P]),
                              wt("ident"), start=True, stop=True)
                last.then_inc(q("ln_spread"), 1)

            eng.wait_ge(q("loaded_x"), 3 * 16)
            for i in range(NCH + 1):
                if i < NCH:
                    if i >= 2:
                        after(eng, "h_ready", 0, i - 1)
                    mm(bank(4 + i % 2, i), wt("proj"), chunk(x, i), start=True, stop=True).then_inc(q("proj_mm"), 1)
                if i == 1:
                    eng.wait_ge(q("loaded_w"), 16)
                    open_rows()
                if i >= 1:
                    after(eng, "h_ready", 0, i)
                    table(0, "edge0_0", h, i - 1)
            eng.wait_ge(q("diag_ready"), 1)
            mm(ps[:, 7, 0:NG], w[0:NG, W_AT["ones"]:W_AT["ones"] + P], base_diag[:], start=True, stop=True)\
                .then_inc(q("base_mm"), 1)
            eng.wait_ge(q("far_lanes"), 1)
            mm(ps[:, 7, 0:1], wt("ones"), far_any[:], start=True, stop=True).then_inc(q("far_lanes_mm"), 1)
            eng.wait_ge(q("loaded_rest"), 16)
            candidate_state(0)
            edge_sums(0)
            eng.wait_ge(q("far_known"), 1)
            far(0)
            after(eng, "added", 0, 1 + NG)
            eng.wait_ge(q("loop_done"), 1)
            open_rows()
            for i in range(NCH + 1):
                if i < NCH:
                    gru(0, i)
                if i >= 1:
                    after(eng, "gru_h", 0, i)
                    table(1, "edge1_0", h, i - 1)
            candidate_state(1)
            eng.wait_ge(q("block_size"), 1)
            mm(ps[0:NB, 6, 0:1], w[0:NB, W_AT["before"]:W_AT["before"] + NB], blk[:, 1:2], start=True, stop=True)\
                .then_inc(q("block_start"), 1)
            eng.wait_ge(q("block_ended"), 1)
            mm(ps[:, 7, 0:ST], w[0:NB, W_AT["ones"]:W_AT["ones"] + P], flat[0:NB, HI1H:HI1H + ST], start=True, stop=True)\
                .then_inc(q("tile_block"), 1)
            edge_sums(1)
            far(1)
            after(eng, "added", 1, 1 + NG)
            eng.wait_ge(q("loop_done"), 2)
            open_rows()
            for i in range(NCH + 3):
                if i < NCH:
                    gru(1, i)
                if 1 <= i < NCH + 1:
                    c = i - 1
                    after(eng, "gru_h", 1, c + 1)
                    if c >= 1:
                        after(eng, "ln_in", 0, c)
                    mm(bank(3, c), wt("out"), chunk(h, c), start=True, stop=True)\
                        .then_inc(q("out_mm"), 1)
                if 2 <= i < NCH + 2:
                    after(eng, "ln_in", 0, i - 1)
                    ln_center(0, i - 2, i % 2)
                if 3 <= i:
                    ln_var(0, i - 3, 2)
            for i in range(NCH + 1):
                if i < NCH:
                    ln_spread(0, i, 6 + i % 2)
                if i >= 1:
                    c = i - 1
                    after(eng, "ln_out", 0, c + 1)
                    table(2, "rel0_0", x, c)
            for c in range(NCH):
                if c >= 2:
                    eng.wait_ge(q("res_used"), c - 1)
                mm(bank(4 + c % 2, c), wt("res"), chunk(x, c), start=True, stop=True).then_inc(q("res_mm"), 1)
            eng.wait_ge(q("res_used"), NCH)
            for k in range(2, 5):
                source = x if k == 2 else h
                if k > 2:
                    for c in range(NCH):
                        after(eng, "h_ready", k - 2, c + 1)
                        if c == 0:
                            open_rows()
                        table(k, f"rel{k - 2}_0", h, c)
                for c in range(NCH):
                    if c >= 2:
                        after(eng, "root_used", k, c - 1)
                    mm(bank(4 + c % 2, c), wt(f"root{k - 2}"), chunk(source, c), start=True, stop=True)\
                        .then_inc(q("root_mm"), 1)
                after(eng, "root_used", k, NCH)
                edge_sums(k)
                far(k)
            for i in range(NCH + 1):
                if i < NCH:
                    after(eng, "ln_in", 1, i + 1)
                    if i == 0:
                        open_rows()
                    ln_center(1, i, i % 2)
                if i >= 1:
                    ln_var(1, i - 1, 2)
            for i in range(NCH + 1):
                if i < NCH:
                    ln_spread(1, i, 6 + i % 2)
                if i >= 1:
                    c = i - 1
                    after(eng, "ln_out", 1, c + 1)
                    if c >= 2:
                        eng.wait_ge(q("gcn_rows"), c - 1)
                    for b in blocks_of(c):
                        last = mm(ps[:, 4 + c % 2, (b % CB) * P:(b % CB + 1) * P], block_of(x, b), wt("gcn"),
                                  start=True, stop=True)
                    last.then_inc(q("gcn_mm"), 1)
            for b in range(TB):
                last = mm(ps[:, 3, b:b + 1], block_of(nodes, b)[32:32 + T], wt("ones")[32:32 + T, 0:1], start=True,
                          stop=True)
            last.then_inc(q("dst_degree_mm"), 1)
            eng.wait_ge(q("gcn_rows"), NCH)
            for c in range(NCH):
                if c >= 2:
                    eng.wait_ge(q("dinv_used"), c - 1)
                for b in blocks_of(c):
                    last = mm(ps[:, 4 + c % 2, (b % CB) * P:(b % CB + 1) * P],
                              dinv[:, b:b + 1].to_broadcast([P, P]), wt("ident"), start=True, stop=True)
                last.then_inc(q("dinv_mm"), 1)
            for c in range(NCH):
                if c >= 2:
                    eng.wait_ge(q("turn_used"), c - 1)
                for b in blocks_of(c):
                    last = mm(ps[SRC_ROWS, 6 + c % 2, (b % CB) * P:(b % CB + 1) * P], by_src[:, b * A:(b + 1) * A],
                              wt("ident"), start=True, stop=True)
                last.then_inc(q("turn_mm"), 1)
            eng.wait_ge(q("dinv_used"), NCH)
            eng.wait_ge(q("turn_used"), NCH)
            eng.wait_ge(q("dst_inv"), 1)
            for c in range(NCH):
                if c >= 2:
                    eng.wait_ge(q("by_dst_mean"), c - 1)
                for b in blocks_of(c):
                    last = mm(ps[:, 4 + c % 2, (b % CB) * P:(b % CB + 1) * P], stat[:, 1, b:b + 1].to_broadcast([P, P]),
                              wt("ident"), start=True, stop=True)
                last.then_inc(q("dst_inv_mm"), 1)
            edge_sums(BY_SRC)
            for i in range(NCH + 1):
                if i < NCH:
                    after(eng, "ln_in", 2, min(i + 2, NCH))
                    ln_center(2, i, 0 if i % 2 else 7)
                if i >= 1:
                    ln_var(2, i - 1, 1)
            for i in range(NCH + 4):
                if i < NCH:
                    ln_spread(2, i, 6 if i % 2 else 2)
                if 1 <= i < NCH + 1:
                    c = i - 1
                    after(eng, "ln_out", 2, c + 1)
                    if c >= 2:
                        eng.wait_ge(q("mlp_pre"), c - 1)
                    mm(bank(5 if c % 2 else 3, c), wt("w1x"), chunk(x, c), start=True, stop=False)
                    mm(bank(5 if c % 2 else 3, c), wt("w1a"), chunk(nodes, c), start=False, stop=True)\
                        .then_inc(q("mlp1_mm"), 1)
                if 2 <= i < NCH + 2:
                    c = i - 2
                    eng.wait_ge(q("mlp_hidden"), c + 1)
                    if c >= 1:
                        after(eng, "ln_in", 3, c)
                    mm(bank(4, c), wt("w2"), tmp[:, 4 + c % 2, 0:width(c)], start=True, stop=True)\
                        .then_inc(q("mlp2_mm"), 1)
                if 3 <= i < NCH + 3:
                    after(eng, "ln_in", 3, i - 2)
                    ln_center(3, i - 3, 7 if i % 2 else 0)
                if i >= 4:
                    ln_var(3, i - 4, 1)
            for c in range(NCH):
                ln_spread(3, c, 6 if c % 2 else 2)

        @block.scalar
        def _(eng):
            act = nc.scalar.activation
            st = Steps(eng, q("act_steps"))

            def table(k, c, some=slice(None)):
                for b in blocks_of(c)[some] if 0 <= c < NCH else ():
                    after(eng, "tab_mm", k, b + 1)
                    if b >= SLOTS:
                        stored(eng, k, b - SLOTS)
                    s = b % SLOTS
                    act(flat[:, s * 1024:s * 1024 + 512], ps[:, 2 * (b % 2), :], ACT.Copy).then_inc(q("tab_act"), 1)

            def stage(k, g, s):
                after(eng, "summed", k, g + 1)
                act(idx_buf[:, s % SUB, :], loops[k][0][:, ds(g * G, G)], ACT.Copy).then_inc(q("idx_staged"), 1)

            def edge_loop(k):
                passes, extra = loops[k][4:]
                ahead = AHEAD if 1 <= k <= 3 else 0
                for s in range(ahead):
                    stage(k, s, s)
                if extra in ("attr_by_src", "scatter"):
                    after(eng, "opened", k, 1)
                with eng.Fori(0, passes) as it:
                    if extra in ("attr_by_src", "scatter"):
                        st.enter(it, SUB)
                    for s in range(SUB):
                        g = it * SUB + s
                        stage(k, g + ahead, s + ahead)
                        if extra == "weigh":
                            eng.wait_ge(q("turned"), g + 1)
                            eng.wait_ge(q("weigh_mm"), g + 1)
                            act(flat[0:T, TT:TT + GE], psf[0:T, 1024:1024 + GE], ACT.Copy)\
                               .then_inc(q("turned_copied"), 1)
                        if extra in ("attr_by_src", "scatter"):
                            lane = src_lo if extra == "attr_by_src" else slot_lane
                            away = tmp[:, 2 * (s % 2):2 * (s % 2) + 2, :].rearrange("p a b -> p (a b)")
                            for t in range(G):
                                last = act(away[:, t * P:(t + 1) * P], iota[:, 0:P], ACT.Abs, scale=-1.0,
                                           bias=lane[:, ds(g * G + t, 1)])
                            st.do(last)
                            after(eng, "extra_used", k, g + 1)
                            act(lane1h[:, s % 2, :, :].rearrange("p a b -> p (a b)"), away, ACT.Relu, scale=-1.0,
                                bias=wt("ones")[:, 0:1]).then_inc(q("lane_ready"), 1)
                    if extra in ("attr_by_src", "scatter"):
                        st.leave(passes)

            def ln_square(r, c, bank_no):
                after(eng, "ln_center", r, c + 1)
                if c >= 2:
                    after(eng, "ln_var", r, c - 1)
                act(tmp[:, c % 2, 0:width(c)], bank(bank_no, c), ACT.Square).then_inc(q("ln_sq"), 1)

            def ln_deviation(r, bank_no):
                after(eng, "ln_var", r, NCH)
                act(stat[:, 0, :], ps[:, bank_no, 0:TB], ACT.Sqrt, bias=bs("eps")).then_inc(q("ln_sd"), 1)

            def gru(l, i, between=lambda some: None):
                if i < NCH:
                    after(eng, "gru_mm", l, i + 1)
                    if i >= 2:
                        after(eng, "gru_mixed", l, i - 1)
                    act(tmp[:, 2 + i % 2, 0:width(i)], bank(4, i), ACT.Sigmoid, bias=bs(f"both{l}_r"))
                    act(tmp[:, 4 + i % 2, 0:width(i)], bank(5, i), ACT.Sigmoid, bias=bs(f"both{l}_z"))\
                        .then_inc(q("gru_rz"), 1)
                    between(slice(0, 1))
                    after(eng, "gru_cand", l, i + 1)
                    act(tmp[:, 6, 0:width(i)], tmp[:, 6, 0:width(i)], ACT.Tanh, bias=bs(f"bih{l}_n"))\
                        .then_inc(q("gru_n"), 1)
                    between(slice(1, 2))
                    after(eng, "gru_mixed", l, i + 1)
                    act(chunk(h, i), tmp[:, 7, 0:width(i)], ACT.Relu).then_inc(q("gru_h"), 1)
                    between(slice(2, None))
                else:
                    between(slice(None))

            eng.wait_ge(q("loaded_x"), 3 * 16)
            for i in range(NCH + 1):
                if i < NCH:
                    eng.wait_ge(q("proj_mm"), i + 1)
                    act(chunk(h, i), bank(4 + i % 2, i), ACT.Relu, bias=bs("proj")).then_inc(q("h_ready"), 1)
                if i >= 1:
                    table(0, i - 1)
            eng.wait_ge(q("rows_ready"), 1)
            edge_loop(0)
            for i in range(NCH + 1):
                gru(0, i, lambda some: table(1, i - 1, some))
            edge_loop(1)
            for i in range(NCH + 2):
                gru(1, i)
                if i >= 2:
                    ln_square(0, i - 2, i % 2)
            ln_deviation(0, 2)
            for c in range(NCH):
                table(2, c)
            for k in range(2, 5):
                if k > 2:
                    for c in range(NCH):
                        table(k, c)
                if k == 3:
                    eng.wait_ge(q("degree"), 1)
                    act(deg[:, 1, :], deg[:, 0, :], ACT.Sqrt).then_inc(q("deg_sqrt"), 1)
                edge_loop(k)
            for i in range(NCH):
                ln_square(1, i, i % 2)
            ln_deviation(1, 2)
            edge_loop(BY_SRC)
            for i in range(NCH):
                ln_square(2, i, 0 if i % 2 else 7)
            ln_deviation(2, 1)
            for i in range(1, NCH + 3):
                if i < NCH + 1:
                    c = i - 1
                    eng.wait_ge(q("mlp1_mm"), c + 1)
                    if c >= 2:
                        eng.wait_ge(q("mlp_hidden"), c - 1)
                    act(tmp[:, 2 + c % 2, 0:width(c)], bank(5 if c % 2 else 3, c), ACT.Identity, bias=bs("mlp1"))\
                        .then_inc(q("mlp_pre"), 1)
                if i >= 3:
                    ln_square(3, i - 3, 7 if i % 2 else 0)
            ln_deviation(3, 1)

        @block.vector
        def _(eng):
            vec = nc.vector
            st = Steps(eng, q("dve_steps"))
            fst = Steps(eng, q("far_dve_steps"))

            def over_tiles(buf, n):
                return buf.unsqueeze(2).to_broadcast([buf.shape[0], buf.shape[1], n])

            def over_lanes(row, n):
                return row.unsqueeze(1).to_broadcast([row.shape[0], n, row.shape[1]])

            def window_starts():
                eng.wait_ge(q("loaded"), 5 * 16)
                st.do(vec.tensor_reduce(first[:], flat[0:NG, 6144:6144 + GE].bitcast(I32), AX.X, ALU.min))
                eng.wait_ge(q("loaded_w"), 16)
                vec.tensor_scalar(base_diag[:], w[0:NG, W_AT["ident"]:W_AT["ident"] + NG], first[:], None, ALU.mult)\
                   .then_inc(q("diag_ready"), 1)
            def rows():
                st.did(vec.tensor_scalar(valid, src[:], float(NONE), None, ALU.is_lt))
                st.did(vec.tensor_copy(typ_f[:, 0:NT], typ[:]))
                st.settle()
                st.did(vec.tensor_scalar(slot_i[:], src[:], P - 1, None, ALU.bitwise_and))
                st.do(vec.scalar_tensor_tensor(out=slot[:], in0=src[:], scalar=float(T), in1=typ_f[:, 0:NT],
                                               op0=ALU.mult, op1=ALU.add))
                st.did(vec.tensor_copy(src_lo[:], slot_i[:]))
                st.did(vec.tensor_tensor(row_idx[:, 0:NT], slot[:], valid, ALU.mult))
                st.settle()
                st.do(vec.tensor_scalar(slot_i[:], src[:], 7, None, ALU.arith_shift_right))
                st.did(vec.tensor_copy(src_hi[:, 0:NT], slot_i[:]))
            def edge_data():
                st.do(vec.tensor_scalar(payload[:], src_lo[:], 1.0, 4096.0, ALU.add, ALU.mult))
                st.do(vec.tensor_tensor(payload[:], payload[:], dst[:], ALU.add))
                st.do(vec.tensor_tensor(payload[:], payload[:], valid, ALU.mult))
                for l in range(2):
                    for g in "rz":
                        st.did(vec.tensor_tensor(bs(f"both{l}_{g}"), bs(f"bih{l}_{g}"), bs(f"bhh{l}_{g}"), ALU.add))
                st.did(vec.memset(nodes[:], 0.0))
                st.did(vec.memset(dst_lo[:, NT:], -1.0))
                st.did(vec.memset(gcn_lo[:, ST:], -1.0))
                st.did(vec.memset(typ_f[:, NT:], 0.0))
                st.did(vec.memset(row_idx[:, NT:], 0))
                st.did(vec.memset(src_hi[:, NT:], 0.0))
                st.did(vec.memset(totals[:, NT:], 0.0))
                st.settle()
                st.did(vec.memset(edge_w[:, NT:], 0.0))

            def windows():
                eng.wait_ge(q("base_mm"), 1)
                st.did(vec.tensor_copy(base_f[:], ps[:, 7, 0:NG]))
                st.did(vec.tensor_copy(base_i[:], ps[:, 7, 0:NG]))
                st.settle()
                st.do(vec.tensor_tensor(by_group(dst_lo[:, 0:NT], G), by_group(dst[:], G), over_tiles(base_f[:], G),
                                        ALU.subtract))
                vec.engine_nop().then_inc(q("rows_ready"), 1)
                st.do(vec.scalar_tensor_tensor(out=slot[:], in0=dst_lo[:, 0:NT], scalar=float(P), in1=valid,
                                               op0=ALU.is_ge, op1=ALU.mult))
                vec.tensor_reduce(far_any[:], slot[:], AX.X, ALU.max).then_inc(q("far_lanes"), 1)
                eng.wait_ge(q("far_lanes_mm"), 1)
                vec.tensor_scalar(far_flag[:], ps[:, 7, 0:1], 1.0, None, ALU.min).then_inc(q("far_known"), 1)

            def table(k, c, some=slice(None)):
                for b in blocks_of(c)[some] if 0 <= c < NCH else ():
                    after(eng, "tab_mm", k, b + 1)
                    if b >= SLOTS:
                        stored(eng, k, b - SLOTS)
                    s = b % SLOTS
                    vec.tensor_copy(flat[:, s * 1024 + 512:(s + 1) * 1024], ps[:, 2 * (b % 2) + 1, :])\
                       .then_inc(q("tab_dve"), 1)

            def edge_sums(k):
                idx, lo, weighted, tab, passes, extra = loops[k]
                last_group = passes * SUB

                def spread(g, s):
                    if weighted:
                        for t in range(G):
                            last = vec.tensor_scalar(onehot[:, s % 2, t, :], iota[:, 0:P], lo[:, ds(g * G + t, 1)],
                                                     edge_w[:, ds(g * G + t, 1)], ALU.is_equal, ALU.mult)
                    else:
                        last = vec.tensor_tensor(onehot[:, s % 2, :, :], over_lanes(iota[:, 0:P], G),
                                                 over_tiles(lo[:, ds(g * G, G)], P), ALU.is_equal)
                    last.then_inc(q("onehot"), 1)

                if k == BY_SRC:
                    vec.memset(flat[:, G * ST:G * ST + 512], 0.0).then_inc(q("zeros"), 1)
                elif k < 2:
                    st.do(vec.memset(acc[:], 0.0))
                else:
                    st.do(vec.memset(acc[:, NV:], 0.0))
                    after(eng, "root_used", k, NCH)
                if k < BY_SRC:
                    all_stored(eng, k)
                if extra in ("attr_by_src", "scatter"):
                    vec.memset(flat[:, G * ST:G * ST + 512], 0.0).then_inc(q("zeros"), 1)
                    after(eng, "opened", k, 1)
                if k == 2:
                    eng.sem_inc(q("extra_ready"), SUB)
                if k != BY_SRC:
                    eng.sem_inc(q("added"), 1)
                if extra == "count":
                    eng.sem_inc(q("counted"), 1)
                if extra == "weigh":
                    eng.sem_inc(q("weighed"), 1)
                def types_ahead(g, s):
                    vec.tensor_tensor(by_group(mark[:, s % SUB, :], TC)[:, :, 0:T],
                                      over_tiles(typ_f[:, ds(g * G, G)], T), over_lanes(iota[:, 0:T], G),
                                      ALU.is_equal).then_inc(q("marked"), 1)
                    vec.tensor_tensor(by_group(rank_diag[s % 2], NB),
                                      over_lanes(w[0:NB, W_AT["ident"]:W_AT["ident"] + NB], G),
                                      over_tiles(totals[:, ds(g * G, G)], NB), ALU.mult).then_inc(q("rank_diag"), 1)
                    st.did(vec.tensor_tensor(by_group(rank1h[s % 2], NB), over_lanes(iota[:, 0:NB], G),
                                             over_tiles(src_hi[:, ds(g * G, G)], NB), ALU.is_equal))

                if extra == "weigh":
                    types_ahead(0, 0)
                    st.settle()
                spread(0, 0)
                with eng.Fori(0, passes) as it:
                    st.enter(it, {"count": 3 * SUB, "weigh": 4 * SUB, "attr_by_src": SUB}.get(extra, 0))
                    for s in range(SUB):
                        g = it * SUB + s
                        if k == BY_SRC:
                            after(eng, "summed", k, g + SUB)
                            spread(g + 1, s + 1)
                            continue
                        base = eng.value_load(base_i[0:1, ds(g, 1)], min_val=0, max_val=NP - P)
                        spread(g + 1, s + 1)
                        if extra == "count":
                            eng.wait_ge(q(f"mark_loaded_{s}"), (it + 1) * 16)
                            vec.tensor_tensor(by_group(mark[:, s, :], TC)[:, :, 0:T],
                                              over_tiles(typ_f[:, ds(g * G, G)], T), over_lanes(iota[:, 0:T], G),
                                              ALU.is_equal).then_inc(q("marked"), 1)
                            vec.tensor_tensor(by_group(rank1h[0], NB), over_lanes(iota[:, 0:NB], G),
                                              over_tiles(src_hi[:, ds(g * G, G)], NB), ALU.is_equal)\
                               .then_inc(q("rank_1h"), 1)
                        if extra == "weigh":
                            types_ahead(g + 1, s + 1)
                        if extra == "attr_by_src":
                            after(eng, "extra_used", k, g + 1)
                            cols = by_group(big[:, s % 2, :], ST)
                            hi1h = cols[:, :, NB * A:MV]
                            st.do(vec.tensor_tensor(hi1h, over_lanes(iota[:, 0:NB], G),
                                                    over_tiles(src_hi[:, ds(g * G, G)], NB), ALU.is_equal))
                            attrs = by_group(mark[:, s, :], TC)[:, :, T:TC]
                            after(eng, f"mark_loaded_{s}", 1, (it + 1) * 16)
                            vec.tensor_tensor(cols[:, :, 0:NB * A].rearrange("p k (b a) -> p k b a", a=A),
                                              hi1h.unsqueeze(3).to_broadcast([P, G, NB, A]),
                                              attrs.unsqueeze(2).to_broadcast([P, G, NB, A]),
                                              ALU.mult).then_inc(q("extra_ready"), 1)
                        if extra == "scatter":
                            after(eng, "extra_used", k, g + 1)
                            for t in range(G):
                                last = vec.tensor_scalar(big[:, s % 2, t * ST:(t + 1) * ST], iota[:, 0:ST],
                                                         slot_tile[:, ds(g * G + t, 1)],
                                                         payload[:, ds(g * G + t, 1)], ALU.is_equal, ALU.mult)
                            last.then_inc(q("extra_ready"), 1)
                        after(eng, "summed", k, g + 1 + SUB)
                        after(eng, "added", k, g + 1)
                        vec.tensor_tensor(acc[:, ds(base, P)], acc[:, ds(base, P)], ps[:, s % 2, 0:P], ALU.add)\
                           .then_inc(q("added"), 1)
                        if extra == "count":
                            eng.wait_ge(q("count_mm"), g + 1 + SUB)
                            eng.wait_ge(q("counted"), g + 1)
                            vec.tensor_tensor(nodes[DST_ROWS, ds(base, P)], nodes[DST_ROWS, ds(base, P)],
                                              ps[DST_ROWS, 2 + s % 2, 0:P], ALU.add).then_inc(q("counted"), 1)
                            eng.wait_ge(q("rank_mm"), g + 1)
                            st.do(vec.tensor_tensor(rank_prod, rank1h[0], ps[:, 4, 0:HW], ALU.mult))
                            st.did(vec.tensor_reduce(slot[:, ds(g * G, G)], by_group(rank_prod, NB), AX.X, ALU.add))
                            st.did(vec.tensor_copy(totals[:, ds(g * G, G)], ps[0:NB, 5, 0:G]))
                            st.settle()
                        if extra == "weigh":
                            eng.wait_ge(q("rank_base"), g + 1)
                            st.do(vec.tensor_tensor(rank_prod, rank1h[s % 2], ps[:, 6 + s % 2, 0:HW], ALU.mult))
                            st.do(vec.tensor_reduce(flat[:, HPROD + 256:HPROD + 256 + G], by_group(rank_prod, NB),
                                                    AX.X, ALU.add))
                            vec.tensor_tensor(slot[:, ds(g * G, G)], slot[:, ds(g * G, G)],
                                              flat[:, HPROD + 256:HPROD + 256 + G], ALU.add)
                            eng.wait_ge(q("weigh_mm"), g + 2)
                            prod = by_group(flat[:, PROD:PROD + GE], P)
                            st.do(vec.tensor_tensor(prod, onehot[:, s % 2, :, :], by_group(psf[:, 2048:2048 + GE], P),
                                                    ALU.mult))
                            vec.tensor_reduce(edge_w[:, ds(g * G, G)], prod, AX.X, ALU.add).then_inc(q("weighed"), 1)
                            eng.wait_ge(q("weighed"), g + 2)
                    st.leave(passes)
                if k == BY_SRC:
                    after(eng, "summed", k, SUB + last_group)
                else:
                    after(eng, "added", k, 1 + last_group)
                if extra == "count":
                    eng.wait_ge(q("counted"), 1 + NG)
                if k != BY_SRC:
                    far(k)
                if k < 2:
                    vec.engine_nop().then_inc(q("loop_done"), 1)

            def far(k):
                idx, lo, weighted, tab, passes, extra = loops[k]
                if k == 0:
                    eng.wait_ge(q("far_known"), 1)
                with eng.If(eng.value_load(far_flag[0:1, 0:1], min_val=0, max_val=1) > 0):
                    eng.sem_inc(q("far_free"), 1)
                    with eng.Fori(0, NG) as g:
                        tiles = ds(g * G, G)
                        with eng.Fori(0, TB) as b:
                            step, block_b = g * TB + b, ds(b * P, P)
                            if extra == "count":
                                eng.wait_ge(q("far_marks"), (g + 1) * 16)
                            fst.enter(step, {"weigh": 7}.get(extra, 5))
                            if k < 2:
                                vec.tensor_tensor(by_group(mark[:, 0, :], TC)[:, :, 0:T], over_tiles(typ_f[:, tiles], T),
                                                  over_lanes(iota[:, 0:T], G), ALU.is_equal)\
                                   .then_inc(q("far_types"), 1)
                            fst.did(vec.tensor_scalar(far_lo[:], lo[:, tiles], base_f[:, ds(g, 1)], None, ALU.add))
                            fst.did(vec.tensor_scalar(far_w[:], lo[:, tiles], float(P), None, ALU.is_ge))
                            fst.settle()
                            fst.do(vec.scalar_tensor_tensor(out=far_lo[:], in0=iota[:, ds(b, 1)].to_broadcast([P, G]),
                                                            scalar=-float(P), in1=far_lo[:], op0=ALU.mult, op1=ALU.add))
                            if weighted:
                                fst.do(vec.tensor_tensor(far_w[:], far_w[:], edge_w[:, tiles], ALU.mult))
                            for t in range(G):
                                last = vec.tensor_scalar(onehot[:, 0, t, :], iota[:, 0:P], far_lo[:, t:t + 1],
                                                         far_w[:, t:t + 1], ALU.is_equal, ALU.mult)
                            last.then_inc(q("far_onehot"), 1)
                            if extra == "weigh":
                                eng.wait_ge(q("far_turned"), step + 1)
                                vec.tensor_copy(flat[0:T, TT:TT + GE], psf[0:T, 1024:1024 + GE])\
                                   .then_inc(q("far_copied"), 1)
                            eng.wait_ge(q("far_mm"), step + (1 + k * FAR_STEPS))
                            fst.did(vec.tensor_tensor(acc[:, block_b], acc[:, block_b], ps[:, 0, 0:P], ALU.add))
                            if extra == "count":
                                fst.did(vec.tensor_tensor(nodes[DST_ROWS, block_b], nodes[DST_ROWS, block_b],
                                                          ps[DST_ROWS, 2, 0:P], ALU.add))
                            if extra == "weigh":
                                prod = by_group(flat[:, PROD:PROD + GE], P)
                                fst.do(vec.tensor_tensor(prod, onehot[:, 0, :, :], by_group(psf[:, 2048:2048 + GE], P),
                                                         ALU.mult))
                                fst.do(vec.tensor_reduce(far_w[:], prod, AX.X, ALU.add))
                                fst.did(vec.tensor_tensor(edge_w[:, tiles], edge_w[:, tiles], far_w[:], ALU.add))
                            fst.settle()
                        eng.sem_inc(q("far_free"), 1)
                    fst.leave(FAR_STEPS)
            def block_starts():
                st.do(vec.tensor_tensor_scan(scanned, totals[:, 0:NT], totals[:, 0:NT], 0.0, ALU.add, ALU.bypass))
                st.do(vec.tensor_scalar(blk[:, 0:1], scanned[:, NT - 1:NT], float(P - 1), None, ALU.add))
                st.do(vec.tensor_copy(blk_i[:, 0:1], blk[:, 0:1]))
                st.do(vec.tensor_scalar(blk_i[:, 1:2], blk_i[:, 0:1], -P, None, ALU.bitwise_and))
                vec.tensor_copy(blk[:, 1:2], blk_i[:, 1:2]).then_inc(q("block_size"), 1)
                eng.wait_ge(q("block_start"), 1)
                st.did(vec.tensor_tensor(blk[:, 3:4], ps[0:NB, 6, 0:1], blk[:, 1:2], ALU.add))
                st.did(vec.tensor_tensor(totals[:, 0:NT], scanned, totals[:, 0:NT], ALU.subtract))
                st.settle()
                st.do(vec.tensor_scalar(totals, totals, ps[0:NB, 6, 0:1], None, ALU.add))
                st.do(vec.tensor_scalar(flat[0:NB, HDIAG:HDIAG + ST], iota[0:NB, 0:ST], float(P), None, ALU.mult))
                vec.tensor_scalar(flat[0:NB, HI1H:HI1H + ST], flat[0:NB, HDIAG:HDIAG + ST], blk[:, 3:4], None,
                                  ALU.is_ge).then_inc(q("block_ended"), 1)
                eng.wait_ge(q("tile_block"), 1)
                st.do(vec.tensor_scalar(gcn_base[:], ps[:, 7, 0:ST], float(P), float(NP - P), ALU.mult, ALU.min))

            def degrees():
                st.do(vec.tensor_copy(by_src[:], ps[:, 7, 0:MV]))
                st.did(vec.tensor_scalar(deg[:, 2, :], by_src[:, NB * A:MV], 0.0, None, ALU.is_gt))
                vec.tensor_scalar(deg[:, 0, :], by_src[:, NB * A:MV], 1.0, None, ALU.max).then_inc(q("degree"), 1)
                eng.wait_ge(q("degree"), 1)
                st.did(vec.reciprocal(deg[:, 3, :], deg[:, 0, :]))
                eng.wait_ge(q("deg_sqrt"), 1)
                st.do(vec.reciprocal(dinv[:], deg[:, 1, :]))
                st.do(vec.tensor_tensor(dinv[:], dinv[:], deg[:, 2, :], ALU.mult))
                sums = by_group(by_src[:, 0:NB * A], A)
                st.do(vec.tensor_tensor(sums, sums, over_tiles(deg[:, 3, :], A), ALU.mult))

            def slots():
                st.do(vec.tensor_copy(slot_i[:], slot[:]))
                st.did(vec.tensor_scalar(src[:], slot_i[:], P - 1, None, ALU.bitwise_and))
                st.did(vec.tensor_scalar(dst[:], slot_i[:], 7, None, ALU.arith_shift_right))
                st.settle()
                st.did(vec.tensor_copy(slot_lane[:], src[:]))
                st.do(vec.tensor_copy(slot_tile[:], dst[:]))

            def sender_order():
                whole = flat[:, HI1H:HI1H + ST].bitcast(I32)
                st.do(vec.tensor_copy(whole, ps[:, 7, 0:ST]))
                st.did(vec.tensor_scalar(gcn_idx[:], whole, 4095, None, ALU.bitwise_and))
                high = flat[:, HDIAG:HDIAG + ST].bitcast(I32)
                st.do(vec.tensor_scalar(high, whole, 12, None, ALU.arith_shift_right))
                st.do(vec.tensor_scalar(gcn_lo[:, 0:ST], high, -1.0, None, ALU.add))

            def root(k):
                for c in range(NCH):
                    after(eng, "root_mm", k, c + 1)
                    vec.tensor_scalar(chunk(acc, c), bank(4 + c % 2, c), bs(f"b{k - 2}"), None, ALU.add)\
                       .then_inc(q("root_used"), 1)

            def keep_state(l):
                for c in range(NCH):
                    after(eng, "state_mm", l, c + 1)
                    vec.tensor_copy(chunk(res, c), bank(4 + c % 2, c)).then_inc(q("state_kept"), 1)

            def gru(l, i, between=lambda some: None):
                if i >= NCH:
                    between(slice(None))
                    return
                n = width(i)
                r, z, cand, new = tmp[:, 2 + i % 2, 0:n], tmp[:, 4 + i % 2, 0:n], tmp[:, 6, 0:n], tmp[:, 7, 0:n]
                after(eng, "gru_rz", l, i + 1)
                st.do(vec.scalar_tensor_tensor(out=cand, in0=chunk(res, i), scalar=bs(f"bhh{l}_n"), in1=r,
                                               op0=ALU.add, op1=ALU.mult))
                vec.tensor_tensor(cand, cand, bank(6, i), ALU.add).then_inc(q("gru_cand"), 1)
                between(slice(0, 2))
                after(eng, "gru_n", l, i + 1)
                if i >= 1:
                    after(eng, "gru_h", l, i)
                st.do(vec.tensor_tensor(new, chunk(h, i), cand, ALU.subtract))
                st.do(vec.tensor_tensor(new, new, z, ALU.mult))
                vec.tensor_tensor(new, new, cand, ALU.add).then_inc(q("gru_mixed"), 1)
                between(slice(2, None))
                after(eng, "gru_mixed", l, i + 1)

            def ln_keep(r, c, bank_no):
                after(eng, "ln_sq", r, c + 1)
                vec.tensor_copy(chunk(acc, c), bank(bank_no, c)).then_inc(q("ln_kept"), 1)

            def ln_invert(r):
                after(eng, "ln_sd", r, 1)
                vec.reciprocal(stat[:, 1, :], stat[:, 0, :]).then_inc(q("ln_rstd"), 1)

            def ln_apply(r, c, bank_no):
                after(eng, "ln_spread", r, c + 1)
                vec.tensor_tensor(chunk(x, c), chunk(acc, c), bank(bank_no, c), ALU.mult).then_inc(q("ln_out"), 1)

            for c, beside in enumerate([window_starts, None, rows] + [None] * (NCH - 3)):
                table(0, c)
                if beside:
                    beside()
            windows()
            edge_data()
            keep_state(0)
            edge_sums(0)
            for i in range(NCH + 1):
                gru(0, i, lambda some: table(1, i - 1, some))
            keep_state(1)
            vec.tensor_copy(nodes[COUNT_ROWS, :], nodes[32:32 + T, :]).then_inc(q("counts_ready"), 1)
            block_starts()
            edge_sums(1)
            for i in range(NCH + 2):
                gru(1, i)
                if 1 <= i < NCH + 1:
                    c = i - 1
                    eng.wait_ge(q("out_mm"), c + 1)
                    vec.scalar_tensor_tensor(out=chunk(acc, c), in0=bank(3, c), scalar=bs("out"), in1=chunk(x, c),
                                             op0=ALU.add, op1=ALU.add).then_inc(q("ln_in"), 1)
                if i >= 2:
                    ln_keep(0, i - 2, i % 2)
            ln_invert(0)
            for i in range(NCH + 1):
                if i < NCH:
                    ln_apply(0, i, 6 + i % 2)
                table(2, i - 1)
            for c in range(NCH):
                eng.wait_ge(q("res_mm"), c + 1)
                vec.tensor_scalar(chunk(res, c), bank(4 + c % 2, c), bs("res"), None, ALU.add)\
                   .then_inc(q("res_used"), 1)
            root(2)
            st.do(vec.tensor_scalar(edge_w[:, 0:NT], edge_w[:, 0:NT], 1.0, None, ALU.max))
            st.do(vec.reciprocal(edge_w[:, 0:NT], edge_w[:, 0:NT]))
            edge_sums(2)
            for k in (3, 4):
                for i in range(NCH + 1):
                    if i < NCH:
                        vec.scalar_tensor_tensor(out=chunk(h, i), in0=chunk(acc, i), scalar=0.0, in1=chunk(res, i),
                                                 op0=ALU.max, op1=ALU.add).then_inc(q("h_ready"), 1)
                    table(k, i - 1)
                root(k)
                if k == 3:
                    degrees()
                    slots()
                else:
                    sender_order()
                edge_sums(k)
            for i in range(NCH + 1):
                if i < NCH:
                    st.do(vec.scalar_tensor_tensor(out=chunk(h, i), in0=chunk(acc, i), scalar=0.0, in1=chunk(res, i),
                                                   op0=ALU.max, op1=ALU.add))
                    vec.tensor_tensor(chunk(acc, i), chunk(h, i), chunk(x, i), ALU.add).then_inc(q("ln_in"), 1)
                if i >= 1:
                    ln_keep(1, i - 1, (i - 1) % 2)
            ln_invert(1)
            for i in range(NCH + 1):
                if i < NCH:
                    ln_apply(1, i, 6 + i % 2)
                if i >= 1:
                    c = i - 1
                    n = len(blocks_of(c))
                    eng.wait_ge(q("gcn_mm"), c + 1)
                    vec.tensor_tensor(by_group(chunk(flat, c), P), by_group(bank(4 + c % 2, c), P),
                                      over_tiles(dinv[:, c * CB:c * CB + n], P), ALU.mult).then_inc(q("gcn_rows"), 1)
            eng.wait_ge(q("dst_degree_mm"), 1)
            st.do(vec.tensor_scalar(stat[:, 0, :], ps[:, 3, 0:TB], 1.0, None, ALU.max))
            vec.reciprocal(stat[:, 1, :], stat[:, 0, :]).then_inc(q("dst_inv"), 1)
            for c in range(NCH):
                eng.wait_ge(q("dinv_mm"), c + 1)
                vec.tensor_copy(chunk(res, c), bank(4 + c % 2, c)).then_inc(q("dinv_used"), 1)
            for c in range(NCH):
                eng.wait_ge(q("turn_mm"), c + 1)
                vec.tensor_copy(chunk(nodes, c)[SRC_ROWS], ps[SRC_ROWS, 6 + c % 2, 0:width(c)])\
                   .then_inc(q("turn_used"), 1)
            for c in range(NCH):
                eng.wait_ge(q("dst_inv_mm"), c + 1)
                vec.tensor_tensor(chunk(nodes, c)[DST_ROWS], chunk(nodes, c)[DST_ROWS], bank(4 + c % 2, c)[DST_ROWS],
                                  ALU.mult).then_inc(q("by_dst_mean"), 1)
            edge_sums(BY_SRC)
            for i in range(NCH + 1):
                for c in (0, 1) if i == 0 else (i + 1,) if i < NCH - 1 else ():
                    st.do(vec.tensor_tensor(chunk(acc, c), bank(c, c), chunk(res, c), ALU.mult))
                    vec.scalar_tensor_tensor(out=chunk(acc, c), in0=chunk(acc, c), scalar=bs("gcn"), in1=chunk(x, c),
                                             op0=ALU.add, op1=ALU.add).then_inc(q("ln_in"), 1)
                if i >= 1:
                    ln_keep(2, i - 1, 7 if i % 2 else 0)
            ln_invert(2)
            for i in range(NCH + 4):
                if i < NCH:
                    ln_apply(2, i, 6 if i % 2 else 2)
                if 1 <= i < NCH + 1:
                    c = i - 1
                    eng.wait_ge(q("mlp_pre"), c + 1)
                    if c >= 2:
                        eng.wait_ge(q("mlp2_mm"), c - 1)
                    pre = tmp[:, 2 + c % 2, 0:width(c)]
                    vec.scalar_tensor_tensor(out=tmp[:, 4 + c % 2, 0:width(c)], in0=pre, scalar=0.01, in1=pre,
                                             op0=ALU.mult, op1=ALU.max).then_inc(q("mlp_hidden"), 1)
                if 2 <= i < NCH + 2:
                    c = i - 2
                    eng.wait_ge(q("mlp2_mm"), c + 1)
                    vec.scalar_tensor_tensor(out=chunk(acc, c), in0=bank(4, c), scalar=bs("mlp2"), in1=chunk(x, c),
                                             op0=ALU.add, op1=ALU.add).then_inc(q("ln_in"), 1)
                if 3 <= i < NCH + 3:
                    ln_keep(3, i - 3, 7 if i % 2 else 0)
            ln_invert(3)
            for c in range(NCH):
                ln_apply(3, c, 6 if c % 2 else 2)


def _layout(v):
    f32 = np.float32

    def tiles(a, fill):
        full = np.full((NT * P,) + a.shape[1:], fill, a.dtype)
        full[:EDGES] = a
        return full

    def lanes(a):
        return np.ascontiguousarray(tiles(a, NONE).reshape(NT, P).T)

    blocks = {"proj": v["L0_gnn_node_proj_w"].T, "out": v["L0_gnn_out_w"].T, "res": v["L1_gnn_res_w"],
              "gcn": v["L2_gnn_W"].T, "w1x": v["L3_gnn_W1"][:P], "w2": v["L3_gnn_W2"]}
    cols = {"proj": v["L0_gnn_node_proj_b"], "out": v["L0_gnn_out_b"], "res": v["L1_gnn_res_b"],
            "gcn": v["L2_gnn_b"], "mlp1": v["L3_gnn_b1"], "mlp2": v["L3_gnn_b2"], "eps": np.full(P, EPS, f32)}
    for l in range(2):
        for t in range(T):
            blocks[f"edge{l}_{t}"] = v["L0_gnn_edge_W"][l, t].T
        for i, g in enumerate("rzn"):
            part = slice(i * P, (i + 1) * P)
            blocks[f"wih{l}_{g}"] = v["L0_gnn_gru_wih"][l, part].T
            blocks[f"whh{l}_{g}"] = v["L0_gnn_gru_whh"][l, part].T
            cols[f"bih{l}_{g}"] = v["L0_gnn_gru_bih"][l, part]
            cols[f"bhh{l}_{g}"] = v["L0_gnn_gru_bhh"][l, part]
    for l in range(3):
        for t in range(T):
            blocks[f"rel{l}_{t}"] = v[f"L1_gnn_W{l + 1}"][t]
        blocks[f"root{l}"] = v[f"L1_gnn_root{l + 1}"]
        cols[f"b{l}"] = v[f"L1_gnn_b{l + 1}"]
    w1a = np.zeros((P, P), f32)
    w1a[SRC_ROWS] = v["L3_gnn_W1"][P:P + A]
    w1a[DST_ROWS.start + T:DST_ROWS.stop] = v["L3_gnn_W1"][P + A:]
    blocks["w1a"] = w1a
    blocks["ident"] = np.eye(P, dtype=f32)
    blocks["mean"] = np.full((P, P), 1 / P, f32)
    blocks["center"] = np.eye(P, dtype=f32) - np.full((P, P), 1 / P, f32)
    blocks["before"] = np.triu(np.ones((P, P), f32), 1)
    blocks["ones"] = np.ones((P, P), f32)

    xT = np.zeros((P, NV), f32)
    xT[:, :NODES] = v["x"].T
    marks = np.zeros((NT * P, TC), f32)
    marks[:EDGES, T:] = v["edge_attr_16"]
    zero = np.zeros(P, f32)
    return {
        "xT": xT, "dst_rows": tiles(v["dst"], NONE).reshape(NG, GE), "dst_lanes": lanes(v["dst"]),
        "src_lanes": lanes(v["src"]), "typ_lanes": lanes(v["edge_type_8"]),
        "marks": np.ascontiguousarray(marks.reshape(NT, P, TC).transpose(1, 0, 2)).reshape(P, NT * TC),
        "weights": np.ascontiguousarray(np.concatenate([blocks[n] for n in W_NAMES], axis=1)),
        "biases": np.ascontiguousarray(np.stack([cols.get(n, zero) for n in B_NAMES], axis=1)),
        "iota": np.ascontiguousarray(np.broadcast_to(np.arange(512, dtype=f32), (P, 512))),
    }


def kernel(**inputs):
    import concourse.bacc as _bacc
    from concourse.bass_utils import run_bass_kernel_spmd as _run

    nc = _bacc.Bacc("TRN2", target_bir_lowering=False, num_devices=1)
    arrays = _layout({k: np.asarray(a) for k, a in inputs.items()})
    args = [nc.dram_tensor(f"in_{n}", a.shape, mybir.dt.from_np(a.dtype), kind="ExternalInput").ap()
            for n, a in arrays.items()]
    args.append(nc.dram_tensor("out_0", (P, NV), F32, kind="ExternalOutput").ap())
    graph_kernel(nc, *args)
    r = _run(nc, [{f"in_{n}": a for n, a in arrays.items()}], core_ids=[0])
    return np.ascontiguousarray(r.results[0]["out_0"][:, :NODES].T)
```
